# Optimizing a Trainium2 kernel written in Bass

```python
import numpy as np
import jax
import jax.numpy as jnp

def _softmax(x, axis=-1):
    return jax.nn.softmax(x, axis=axis)

def _gelu(x):
    return jax.nn.gelu(x, approximate=True)

def _silu(x):
    return jax.nn.silu(x)

def _sigmoid(x):
    return jax.nn.sigmoid(x)

def _layernorm(x, axis=-1, eps=1e-05):
    m = jnp.mean(x, axis=axis, keepdims=True)
    v = jnp.var(x, axis=axis, keepdims=True)
    return (x - m) / jnp.sqrt(v + eps)

def _scatter_add(tgt, idx, src, axis=0):
    return tgt.at[idx].add(src)

def _segment_sum(src, seg, n):
    return jax.ops.segment_sum(src, seg, n)
kernel_name = 'mk_sandwich_d1_jaxref_r4_15874d'

def setup_inputs(seed: int=0):
    np.random.seed(seed)
    _w = jnp.asarray

    def _L0_attn_setup():
        import jax, jax.numpy as jnp
        import numpy as np
        import math
        D_MODEL = 1024
        NUM_HEADS = 32
        NUM_KV_HEADS = 8
        HEAD_DIM = D_MODEL // NUM_HEADS
        GROUP = NUM_HEADS // NUM_KV_HEADS
        SEQ_LEN = 512
        BATCH = 2
        ROPE_THETA = 10000.0

        def apply_rope(x, start_pos=0):
            b, h, s, hd = x.shape
            inv_freq = 1.0 / ROPE_THETA ** (jnp.arange(0, hd, 2, dtype=jnp.float32) / hd)
            pos = jnp.arange(start_pos, start_pos + s, dtype=jnp.float32)
            ang = pos[:, None] * inv_freq[None, :]
            cos = jnp.cos(ang).astype(x.dtype)
            sin = jnp.sin(ang).astype(x.dtype)
            xr = x[..., 0::2]
            xi = x[..., 1::2]
            out_r = xr * cos - xi * sin
            out_i = xr * sin + xi * cos
            return jnp.stack([out_r, out_i], axis=-1).reshape(b, h, s, hd)
        key = jax.random.key(seed)
        ks = jax.random.split(key, 5)
        qkv_dim = HEAD_DIM * (NUM_HEADS + 2 * NUM_KV_HEADS)
        scale = 1.0 / math.sqrt(D_MODEL)
        return {'x': jax.random.normal(ks[0], (BATCH, SEQ_LEN, D_MODEL), jnp.float32), 'w_qkv': jax.random.normal(ks[1], (qkv_dim, D_MODEL), jnp.float32) * scale, 'b_qkv': jax.random.normal(ks[2], (qkv_dim,), jnp.float32) * 0.01, 'w_o': jax.random.normal(ks[3], (D_MODEL, D_MODEL), jnp.float32) * scale, 'b_o': jax.random.normal(ks[4], (D_MODEL,), jnp.float32) * 0.01}
    _L0_attn_in = _L0_attn_setup()

    def _L0_ffn_setup():
        import jax, jax.numpy as jnp
        import numpy as np
        B, S, D_IN, D_OUT = (2, 512, 1024, 1024)
        E, K, R = (8, 2, 16)
        SCALING = 32.0 / 16.0
        key = jax.random.key(seed)
        ks = jax.random.split(key, 6)
        x = jax.random.normal(ks[0], (B, S, D_IN), dtype=jnp.float32)
        gate_w = jax.random.normal(ks[1], (E, D_IN), dtype=jnp.float32) * 0.02
        base_w = jax.random.normal(ks[2], (D_OUT, D_IN), dtype=jnp.float32) * 0.02
        base_b = jax.random.normal(ks[3], (D_OUT,), dtype=jnp.float32) * 0.02
        lora_A = jax.random.normal(ks[4], (E, R, D_IN), dtype=jnp.float32) * 0.02
        lora_B = jax.random.normal(ks[5], (E, D_OUT, R), dtype=jnp.float32) * 0.02
        return {'x': x, 'gate_w': gate_w, 'base_w': base_w, 'base_b': base_b, 'lora_A': lora_A, 'lora_B': lora_B}
    _L0_ffn_in = _L0_ffn_setup()
    _d = {'L0_attn_x': _L0_attn_in['x'], 'L0_attn_w_qkv': _L0_attn_in['w_qkv'], 'L0_attn_b_qkv': _L0_attn_in['b_qkv'], 'L0_attn_w_o': _L0_attn_in['w_o'], 'L0_attn_b_o': _L0_attn_in['b_o'], 'L0_ffn_gate_w': _L0_ffn_in['gate_w'], 'L0_ffn_base_w': _L0_ffn_in['base_w'], 'L0_ffn_base_b': _L0_ffn_in['base_b'], 'L0_ffn_lora_A': _L0_ffn_in['lora_A'], 'L0_ffn_lora_B': _L0_ffn_in['lora_B']}
    _x0 = _d['L0_attn_x']
    _d['L0_attn_x'] = jax.random.normal(jax.random.fold_in(jax.random.key(seed), 1), (4, 512, 1024), dtype=_x0.dtype)
    del _x0
    return _d

def reference(L0_attn_x, L0_attn_w_qkv, L0_attn_b_qkv, L0_attn_w_o, L0_attn_b_o, L0_ffn_gate_w, L0_ffn_base_w, L0_ffn_base_b, L0_ffn_lora_A, L0_ffn_lora_B):

    def _L0_attn_ref(x, w_qkv, b_qkv, w_o, b_o):
        import jax, jax.numpy as jnp
        import numpy as np
        import math
        D_MODEL = 1024
        NUM_HEADS = 32
        NUM_KV_HEADS = 8
        HEAD_DIM = D_MODEL // NUM_HEADS
        GROUP = NUM_HEADS // NUM_KV_HEADS
        SEQ_LEN = 512
        BATCH = 2
        ROPE_THETA = 10000.0

        def apply_rope(x, start_pos=0):
            b, h, s, hd = x.shape
            inv_freq = 1.0 / ROPE_THETA ** (jnp.arange(0, hd, 2, dtype=jnp.float32) / hd)
            pos = jnp.arange(start_pos, start_pos + s, dtype=jnp.float32)
            ang = pos[:, None] * inv_freq[None, :]
            cos = jnp.cos(ang).astype(x.dtype)
            sin = jnp.sin(ang).astype(x.dtype)
            xr = x[..., 0::2]
            xi = x[..., 1::2]
            out_r = xr * cos - xi * sin
            out_i = xr * sin + xi * cos
            return jnp.stack([out_r, out_i], axis=-1).reshape(b, h, s, hd)
        bs, seq_len, d_model = x.shape
        qkv = x @ w_qkv.T + b_qkv
        q_dim = NUM_HEADS * HEAD_DIM
        kv_dim = NUM_KV_HEADS * HEAD_DIM
        q, k, v = jnp.split(qkv, [q_dim, q_dim + kv_dim], axis=-1)
        q = q.reshape(bs, seq_len, NUM_HEADS, HEAD_DIM).transpose(0, 2, 1, 3)
        k = k.reshape(bs, seq_len, NUM_KV_HEADS, HEAD_DIM).transpose(0, 2, 1, 3)
        v = v.reshape(bs, seq_len, NUM_KV_HEADS, HEAD_DIM).transpose(0, 2, 1, 3)
        q = apply_rope(q, 0)
        k = apply_rope(k, 0)
        k = jnp.repeat(k, GROUP, axis=1)
        v = jnp.repeat(v, GROUP, axis=1)
        scores = jnp.einsum('bhqd,bhkd->bhqk', q, k) / math.sqrt(HEAD_DIM)
        causal = jnp.tril(jnp.ones((seq_len, seq_len), dtype=bool))
        scores = jnp.where(causal[None, None, :, :], scores, jnp.float32(-1e+20))
        attn = jax.nn.softmax(scores, axis=-1)
        out = jnp.einsum('bhqk,bhkd->bhqd', attn, v)
        out = out.transpose(0, 2, 1, 3).reshape(bs, seq_len, d_model)
        return out @ w_o.T + b_o

    def _L0_ffn_ref(x, gate_w, base_w, base_b, lora_A, lora_B):
        import jax, jax.numpy as jnp
        import numpy as np
        B, S, D_IN, D_OUT = (2, 512, 1024, 1024)
        E, K, R = (8, 2, 16)
        SCALING = 32.0 / 16.0
        gate_logits = jnp.einsum('bsd,ed->bse', x, gate_w)
        weights, selected = jax.lax.top_k(gate_logits, K)
        weights = jax.nn.softmax(weights.astype(jnp.float32), axis=2).astype(x.dtype)
        result = jnp.einsum('bsd,od->bso', x, base_w) + base_b
        w_full = jnp.sum(jax.nn.one_hot(selected, E, dtype=x.dtype) * weights[..., None], axis=2)
        low = jnp.einsum('bsd,erd->ebsr', x, lora_A)
        lora_out = jnp.einsum('ebsr,eor,bse->bso', low, lora_B, w_full)
        result = result + SCALING * lora_out
        return result
    x = L0_attn_x
    x = x + _layernorm(_L0_attn_ref(_layernorm(x, axis=-1), L0_attn_w_qkv, L0_attn_b_qkv, L0_attn_w_o, L0_attn_b_o), axis=-1)
    x = x + _layernorm(_L0_ffn_ref(_layernorm(x, axis=-1), L0_ffn_gate_w, L0_ffn_base_w, L0_ffn_base_b, L0_ffn_lora_A, L0_ffn_lora_B), axis=-1)
    return x

_drawn_inputs = setup_inputs


def setup_inputs(seed=0):
    import zlib

    import numpy as np

    out = dict(_drawn_inputs(seed))
    spreads = {}
    factors = {'L0_ffn_base_b': 3.351}
    for name, (base, spread) in spreads.items():
        noise = np.random.default_rng([zlib.crc32(name.encode()), seed]).standard_normal(out[name].shape)
        drawn = base * np.exp(spread * noise) if base else spread * noise
        out[name] = jnp.asarray(drawn.astype(out[name].dtype))
    for name, factor in factors.items():
        out[name] = (out[name] * factor).astype(out[name].dtype)
    return out
```

```python
from contextlib import ExitStack

import concourse.bass as bass
from concourse import mybir

F32 = mybir.dt.float32
F32R = mybir.dt.float32r
BF16 = mybir.dt.bfloat16
ALU = mybir.AluOpType
ACT = mybir.ActivationFunctionType
AX_X = mybir.AxisListType.X

P = 128
D = 1024
KC = D // P
BATCH, SEQ = 4, 512
NT = BATCH * SEQ // P
TT = SEQ // P
HEADS, KV, HD = 32, 8, 32
REP = HEADS // KV
GW = (REP + 2) * HD
QKW = (REP + 1) * HD
QKV = KV * GW
NG = BATCH * KV
EXP, RANK = 8, 16
ER = EXP * RANK
AGW = EXP + ER
FW = AGW + D
EPS = 1e-5
SCALING = 2.0
INV_SQRT_HD = float(HD) ** -0.5
HALF = 512
MASKED = -1.0e30
ST = 3 * HD
OUT_SPLIT = (KC + 1) * D
PIECE = OUT_SPLIT // NG
FFN_COLS = [(0, AGW + 256), (AGW + 256, 384), (AGW + 640, 384)]
WQ_RING = 4


def wait(eng, sem, value):
    if not (isinstance(value, int) and value <= 0):
        eng.wait_ge(sem, value)


def wait_apart(eng, sem, value, passed):
    if not (isinstance(value, int) and value <= 0):
        if not isinstance(value, int):
            eng.compute_val(value)
            eng.wait_ge(*passed)
        eng.wait_ge(sem, value)


def live(n, lo, hi):
    return not isinstance(n, int) or lo <= n < hi


def run_steps(eng, first, lo, hi, last, step):
    for n in range(first, lo):
        step(n, n % 2)
    with eng.Fori(lo // 2, hi // 2) as i:
        for j in range(2):
            step(2 * i + j, j)
    for n in range(hi, last):
        step(n, n % 2)


def build(nc, x, w_qkv, b_qkv, w_out, b_o, w_ffn, b_ffn, cos_t, sin_t, ident_h, causal_h, before_h, out):
    qkv_scratch = nc.dram_tensor("qkv_scratch", [NT, P, QKV], F32).ap()
    att_scratch = nc.dram_tensor("att_scratch", [NG // KV, KV, P, SEQ], F32).ap()

    with ExitStack() as ctx:
        arena = ctx.enter_context(nc.sbuf_tensor("arena", [P, 212000], mybir.dt.uint8))
        del arena
        start = 16640
        limit = 16512 + 212000

        def sem(name):
            return ctx.enter_context(nc.semaphore(name))

        class Map:

            def __init__(self, at):
                self.at = at

            def __call__(self, name, shape, dtype=F32):
                size = mybir.dt.size(dtype)
                for n in shape[1:]:
                    size *= n
                t = nc.alloc_sbuf_tensor_at(name, shape, dtype, offset=self.at)
                self.at += -(-size // 32) * 32
                assert self.at <= limit, (name, self.at - limit)
                return t

        m = Map(start)
        ident = m("ident", [P, P])
        ident_r = m("ident_r", [P, P], F32R)
        ident_b = m("ident_b", [P, P], BF16)
        causal_b = m("causal_b", [P, P], BF16)
        causal = m("causal", [P, P])
        ones = m("ones", [P, HD])
        before = m("before", [P, EXP, EXP])
        bo_row = m("bo_row", [P, D])
        bf_row = m("bf_row", [P, D])
        ln_st = [m(f"ln_st{j}", [P, 2, 6]) for j in range(2)]
        ln_mv = [m(f"ln_mv{j}", [P, 2]) for j in range(2)]
        ln_rs = [m(f"ln_rs{j}", [P, 1]) for j in range(2)]
        ln_nm = [m(f"ln_nm{j}", [P, 1]) for j in range(2)]
        ln_ve = [m(f"ln_ve{j}", [P, 1]) for j in range(2)]
        ln_mm = [m(f"ln_mm{j}", [P, 1]) for j in range(2)]
        minus_half = m("minus_half", [P, 1])
        minus_one = m("minus_one", [P, 1])
        eps_col = m("eps_col", [P, 1])
        common_end = m.at

        wq_h = m("wq_h", [P, KC, QKV], F32R)
        wq_l = m("wq_l", [P, KC, QKV], F32R)
        wq_raw = [m(f"wq_raw{j}", [P, QKV]) for j in range(WQ_RING)]
        x_in = [m(f"x_in{j}", [P, D]) for j in range(2)]
        xn = [m(f"xn{j}", [P, D]) for j in range(2)]
        xt_h = [m(f"xt_h{j}", [P, KC, P], F32R) for j in range(2)]
        xt_l = [m(f"xt_l{j}", [P, KC, P], F32R) for j in range(2)]
        qkv = [m(f"qkv{j}", [P, KV, GW]) for j in range(2)]
        rope_c = m("rope_c", [P, KV, REP + 1, HD])
        rope_s = m("rope_s", [P, KV, REP + 1, HD])
        bq_row = m("bq_row", [P, QKV])
        cos_sb = m("cos_sb", [P, TT, HD])
        sin_sb = m("sin_sb", [P, TT, HD])

        m = Map(common_end)
        wo_h = m("wo_h", [P, OUT_SPLIT], F32R)
        wo_l = m("wo_l", [P, OUT_SPLIT], F32R)
        out_end = m.at
        wo_raw = [m(f"wo_raw{j}", [P, PIECE]) for j in range(2)]
        grp = [m(f"grp{j}", [P, TT, GW]) for j in range(2)]
        v_sb = [m(f"v_sb{j}", [P, TT, HD]) for j in range(2)]
        stack = [m(f"stack{j}", [P, TT, REP + 1, ST], F32R) for j in range(2)]
        q_t = [m(f"q_t{j}", [P, REP, SEQ], F32R) for j in range(2)]
        k_t = [m(f"k_t{j}", [P, SEQ], F32R) for j in range(2)]
        prob = [m(f"prob{j}", [P, REP, 1408]) for j in range(2)]
        neg_max = m("neg_max", [P, TT, REP])
        shift = m("shift", [P, TT, REP, HD], F32R)
        den_t = m("den_t", [P, SEQ])
        den_r = m("den_r", [P, SEQ // HD])
        den_i = m("den_i", [P, SEQ])
        att = [m(f"att{j}", [P, SEQ]) for j in range(2)]

        m = Map(out_end)
        wf_h = m("wf_h", [P, KC, FW], F32R)
        wf_l = m("wf_l", [P, KC, FW], F32R)
        att_in = m("att_in", [P, KC, P])
        at_h = m("at_h", [P, KC, P], F32R)
        at_l = m("at_l", [P, KC, P], F32R)
        x_res = m("x_res", [P, D])
        y = m("y", [P, D])
        x1 = [m(f"x1_{j}", [P, D]) for j in range(2)]
        xt2_h = m("xt2_h", [P, KC, P], F32R)
        xt2_l = m("xt2_l", [P, KC, P], F32R)
        raw_at = m.at
        z = [m(f"z{j}", [P, D]) for j in range(2)]
        low = m("low", [P, EXP, RANK])
        low_h = m("low_h", [P, P], F32R)
        low_l = m("low_l", [P, P], F32R)
        raw_end = m.at
        logit = m("logit", [P, EXP])
        later = m("later", [P, EXP, EXP])
        equal = m("equal", [P, EXP, EXP])
        rank = m("rank", [P, EXP])
        neg_top = m("neg_top", [P, 1])
        gate_e = m("gate_e", [P, EXP])
        gate_w = m("gate_w", [P, EXP])
        gate_s = m("gate_s", [P, 1])
        gate_r = m("gate_r", [P, 1])
        m = Map(raw_at)
        raw_f = [m(f"raw_f{j}", [P, FW]) for j in range(2)]
        assert m.at <= raw_end

        bank = [ctx.enter_context(nc.psum_tensor(f"bank{i}", [P, HALF], F32)) for i in range(8)]

        row_loaded = sem("row_loaded")
        const_ready = sem("const_ready")
        wq_loaded = [sem(f"wq_loaded{j}") for j in range(WQ_RING)]
        wq_hi = sem("wq_hi")
        wq_ready = sem("wq_ready")
        x_loaded = [sem(f"x_loaded{j}") for j in range(2)]
        ln1_step = sem("ln1_step")
        ln1_norm = sem("ln1_norm")
        half_set = sem("half_set")
        xn_ready = sem("xn_ready")
        xt_ps = sem("xt_ps")
        xt_hi = sem("xt_hi")
        xt_ready = sem("xt_ready")
        proj_ps = sem("proj_ps")
        qkv_step = sem("qkv_step")
        qkv_stored = [sem(f"qkv_stored{j}") for j in range(2)]
        grp_loaded = [sem(f"grp_loaded{j}") for j in range(2)]
        v_loaded = [sem(f"v_loaded{j}") for j in range(2)]
        wo_loaded = [sem(f"wo_loaded{j}") for j in range(2)]
        wo_hi = sem("wo_hi")
        wo_ready = sem("wo_ready")
        split_hi = sem("split_hi")
        split_lo = sem("split_lo")
        stack_ps = sem("stack_ps")
        stack_sb = sem("stack_sb")
        row_ps = sem("row_ps")
        row_max = sem("row_max")
        shift_step = sem("shift_step")
        shift_ps = sem("shift_ps")
        shift_sb = sem("shift_sb")
        score_ps = sem("score_ps")
        prob_ready = sem("prob_ready")
        prob_masked = sem("prob_masked")
        den_ps = sem("den_ps")
        den_step = sem("den_step")
        pv_ps = sem("pv_ps")
        att_ready = sem("att_ready")
        att_stored = [sem(f"att_stored{j}") for j in range(2)]
        wf_loaded = [sem(f"wf_loaded{j}") for j in range(2)]
        wf_hi = sem("wf_hi")
        wf_ready = sem("wf_ready")
        att_loaded = sem("att_loaded")
        res_loaded = sem("res_loaded")
        at_hi = sem("at_hi")
        at_ready = sem("at_ready")
        o_ps = sem("o_ps")
        y_step = sem("y_step")
        y_scale = sem("y_scale")
        y_norm = sem("y_norm")
        xt2_ps = sem("xt2_ps")
        xt2_hi = sem("xt2_hi")
        xt2_ready = sem("xt2_ready")
        ffn_ps = sem("ffn_ps")
        gate_step = sem("gate_step")
        gate_exp = sem("gate_exp")
        low_ps = sem("low_ps")
        low_hi = sem("low_hi")
        low_ready = sem("low_ready")
        lora_ps = sem("lora_ps")
        z_step = sem("z_step")
        z_scale = sem("z_scale")
        z_norm = sem("z_norm")
        out_stored = [sem(f"out_stored{j}") for j in range(2)]

        block = ctx.enter_context(nc.Block())

        N_ROWS = 8
        FIRST_X = (x_loaded[0], 16)

        def phase1_done(eng):
            eng.wait_ge(proj_ps, 3 * NT)
            eng.wait_ge(qkv_step, 7 * NT)
            for j in range(2):
                eng.wait_ge(qkv_stored[j], 16 * (NT // 2))

        def phase2_done(eng):
            eng.wait_ge(pv_ps, NG)
            eng.wait_ge(att_ready, NG)
            eng.wait_ge(wo_ready, NG)
            for j in range(2):
                eng.wait_ge(att_stored[j], 16 * (NG // 2))

        @block.sync
        def _(sp):
            sp.dma_start(x_in[0][:], x[0]).then_inc(x_loaded[0], 16)
            sp.dma_start(ident[:], ident_h).then_inc(row_loaded, 16)
            sp.dma_start(wq_raw[0][:], w_qkv[:, 0, :]).then_inc(wq_loaded[0], 16)
            sp.dma_start(x_in[1][:], x[1]).then_inc(x_loaded[1], 16)
            for c in range(1, WQ_RING):
                sp.dma_start(wq_raw[c][:], w_qkv[:, c, :]).then_inc(wq_loaded[c], 16)
            sp.dma_start(bq_row[:], b_qkv[0].partition_broadcast(P)).then_inc(row_loaded, 16)
            sp.dma_start(cos_sb[:], cos_t).then_inc(row_loaded, 16)
            sp.dma_start(sin_sb[:], sin_t).then_inc(row_loaded, 16)
            sp.dma_start(causal[:], causal_h).then_inc(row_loaded, 16)
            sp.dma_start(before[:], before_h[0].partition_broadcast(P)).then_inc(row_loaded, 16)
            sp.dma_start(bo_row[:], b_o[0].partition_broadcast(P)).then_inc(row_loaded, 16)
            sp.dma_start(bf_row[:], b_ffn[0].partition_broadcast(P)).then_inc(row_loaded, 16)
            for c in range(WQ_RING, KC):
                sp.wait_ge(wq_ready, c - WQ_RING + 1)
                sp.dma_start(wq_raw[c % WQ_RING][:], w_qkv[:, c, :]).then_inc(wq_loaded[c % WQ_RING], 16)

            def io1(t, j):
                if live(t + 2, 0, NT):
                    wait_apart(sp, xn_ready, t + 1, FIRST_X)
                    sp.dma_start(x_in[j][:], x[t + 2]).then_inc(x_loaded[j], 16)
                wait_apart(sp, qkv_step, 7 * t + 7, FIRST_X)
                sp.dma_start(qkv_scratch[t], qkv[j][:].rearrange("p g c -> p (g c)")).then_inc(qkv_stored[j], 16)

            run_steps(sp, 0, 0, NT - 2, NT, io1)

            phase1_done(sp)

            def group(n):
                return n // KV, n % KV

            def load_group(n, j):
                b, g = group(n)
                wait_apart(sp, split_hi, 3 * (n - 1), FIRST_X)
                wait(sp, split_lo, 2 * (n - 1))
                src = qkv_scratch.rearrange("(b t) p (g c) -> b g p t c", t=TT, c=GW)[b, g]
                sp.dma_start(grp[j][:], src).then_inc(grp_loaded[j], 16)

            def load_v(n, j):
                b, g = group(n)
                wait_apart(sp, pv_ps, n - 1, FIRST_X)
                src = qkv_scratch.rearrange("(b t) p (g c) -> b g p t c", t=TT, c=GW)[b, g][:, :, QKW:GW]
                sp.dma_start(v_sb[j][:], src).then_inc(v_loaded[j], 16)

            def load_piece(n, j):
                wait_apart(sp, wo_ready, n - 1, FIRST_X)
                src = w_out.rearrange("p (n c) -> n p c", c=PIECE)[n]
                sp.dma_start(wo_raw[j][:], src).then_inc(wo_loaded[j], 16)

            def store_att(n, j):
                b, g = group(n)
                wait_apart(sp, att_ready, n + 1, FIRST_X)
                sp.dma_start(att_scratch[b, g], att[j][:]).then_inc(att_stored[j], 16)

            def io2(n, j):
                if live(n + 2, 0, NG):
                    load_group(n + 2, j)
                if live(n + 1, 2, NG):
                    load_v(n + 1, 1 - j)
                if live(n, 0, NG):
                    load_piece(n, j)
                if live(n - 1, 0, NG):
                    store_att(n - 1, 1 - j)

            load_group(0, 0)
            load_group(1, 1)
            load_v(0, 0)
            load_v(1, 1)
            run_steps(sp, 0, 2, NG - 2, NG + 1, io2)

            phase2_done(sp)

            def load_tile(t):
                wait_apart(sp, at_ready, t, FIRST_X)
                src = att_scratch.rearrange("b g p (t c) -> b t p g c", c=P)[t // TT, t % TT]
                sp.dma_start(att_in[:], src).then_inc(att_loaded, 16)
                wait_apart(sp, y_step, 9 * (t - 1) + 6, FIRST_X)
                sp.dma_start(x_res[:], x[t]).then_inc(res_loaded, 16)

            def load_ffn(c):
                wait(sp, wf_ready, c - 1)
                sp.dma_start(raw_f[c % 2][:], w_ffn[:, c, :]).then_inc(wf_loaded[c % 2], 16)

            def store_out(t, j):
                wait_apart(sp, z_step, 7 * t + 7, FIRST_X)
                sp.dma_start(out[t], z[j][:]).then_inc(out_stored[j], 16)

            def io3(t, j):
                if live(t - 1, 0, NT):
                    store_out(t - 1, 1 - j)
                if live(t + 2, 0, NT):
                    load_tile(t + 2)

            load_tile(0)
            load_ffn(0)
            load_ffn(1)
            for c in range(2, KC):
                load_ffn(c)
            load_tile(1)
            run_steps(sp, 0, 2, NT - 2, NT + 1, io3)
            for j in range(2):
                sp.wait_ge(out_stored[j], 16 * (NT // 2))

        @block.gpsimd
        def _(pool):
            def scale_and_shift(j, count, before_it):
                nc.gpsimd.tensor_tensor(ln_ve[j][:], ln_mv[j][:, 1:2], eps_col[:], ALU.add).then_inc(count, 1)
                nc.gpsimd.tensor_tensor(ln_mm[j][:], ln_mv[j][:, 0:1], minus_one[:], ALU.mult).then_inc(count, 1)
                pool.wait_ge(count, before_it + 1)
                nc.gpsimd.tensor_tensor(ln_rs[j][:], ln_ve[j][:], minus_half[:], ALU.pow).then_inc(count, 1)
                pool.wait_ge(count, before_it + 3)
                nc.gpsimd.tensor_tensor(ln_nm[j][:], ln_mm[j][:], ln_rs[j][:], ALU.mult).then_inc(count, 1)

            def scale1(t, j):
                pool.wait_ge(ln1_step, 3 * t + 3)
                scale_and_shift(j, ln1_norm, 4 * t)

            nc.gpsimd.memset(minus_half[:], -0.5).then_inc(half_set, 1)
            nc.gpsimd.memset(minus_one[:], -1.0).then_inc(half_set, 1)
            nc.gpsimd.memset(eps_col[:], EPS).then_inc(half_set, 1)
            pool.wait_ge(half_set, 3)
            run_steps(pool, 0, 2, NT, NT, scale1)

            phase1_done(pool)

            def mask(n, j):
                for h in range(REP):
                    wait_apart(pool, prob_ready, 12 * n + 3 * h + 3, (half_set, 3))
                    d0 = prob[j][:, h, 0:P]
                    nc.gpsimd.affine_select(out=d0, in_=d0, compare_op=ALU.is_ge, fill=0.0, base=0,
                                            pattern=[[1, P]], channel_multiplier=-1).then_inc(prob_masked, 1)
                    d1 = prob[j][:, h, 512:1408].rearrange("p (a c) -> p a c", c=P)[:, 0:7:3, :]
                    nc.gpsimd.affine_select(out=d1, in_=d1, compare_op=ALU.is_ge, fill=0.0, base=0,
                                            pattern=[[0, 3], [1, P]], channel_multiplier=-1).then_inc(prob_masked, 1)

            def split_piece(n, j):
                wait_apart(pool, wo_loaded[j], 16 * (n // 2) + 16, (half_set, 3))
                hi = wo_h[:, bass.ds(n * PIECE, PIECE)]
                lo = wo_l[:, bass.ds(n * PIECE, PIECE)]
                nc.gpsimd.tensor_copy(hi, wo_raw[j][:]).then_inc(wo_hi, 1)
                pool.wait_ge(wo_hi, n + 1)
                nc.gpsimd.tensor_tensor(lo, wo_raw[j][:], hi.bitcast(F32), ALU.subtract).then_inc(wo_ready, 1)

            def split_group(n, j):
                pool.wait_ge(split_hi, 3 * n + 3)
                qk = grp[j][:, :, 0:QKW].rearrange("p t (h c) -> p t h c", c=HD)
                hi = stack[j][:, :, :, 0:HD].bitcast(F32)
                nc.gpsimd.tensor_tensor(stack[j][:, :, 0:REP, HD:2 * HD], qk[:, :, 0:REP, :], hi[:, :, 0:REP, :],
                                        ALU.subtract).then_inc(split_lo, 1)
                nc.gpsimd.tensor_tensor(stack[j][:, :, REP, 2 * HD:ST], qk[:, :, REP, :], hi[:, :, REP, :],
                                        ALU.subtract).then_inc(split_lo, 1)

            def step2(n, j):
                if live(n + 2, 0, NG):
                    split_group(n + 2, j)
                if live(n, 0, NG):
                    split_piece(n, j)
                    mask(n, j)

            split_group(0, 0)
            run_steps(pool, -1, 2, NG - 2, NG, step2)

            phase2_done(pool)

            def scale_y(t):
                pool.wait_ge(y_step, 9 * t + 5)
                scale_and_shift(0, y_scale, 8 * t)
                pool.wait_ge(y_step, 9 * t + 9)
                scale_and_shift(0, y_scale, 8 * t + 4)

            def scale_z(t):
                pool.wait_ge(z_step, 7 * t + 6)
                scale_and_shift(1, z_scale, 4 * t)

            def step3(t, j):
                if live(t - 1, 0, NT):
                    scale_z(t - 1)
                if live(t + 1, 0, NT):
                    scale_y(t + 1)

            scale_y(0)
            run_steps(pool, 0, 2, NT - 2, NT + 1, step3)

        @block.scalar
        def _(act):
            def normalise1(t, j):
                act.wait_ge(ln1_norm, 4 * t + 4)
                wait(act, xt_ps, t - 1)
                nc.scalar.activation(xn[j][:], x_in[j][:], ACT.Identity, bias=ln_nm[j][:], scale=ln_rs[j][:]
                                     ).then_inc(xn_ready, 1)

            def transposed1(t, j):
                wait(act, proj_ps, 3 * (t - 1))
                act.wait_ge(xt_ps, t + 1)
                for h in range(2):
                    last = nc.scalar.copy(xt_h[j][:, 4 * h:4 * h + 4, :].rearrange("p c t -> p (c t)"), bank[h][:])
                last.then_inc(xt_hi, 1)

            def step1(t, j):
                if live(t + 1, 0, NT):
                    transposed1(t + 1, 1 - j)
                if live(t + 2, 0, NT):
                    normalise1(t + 2, j)

            normalise1(0, 0)
            for c in range(KC):
                act.wait_ge(wq_loaded[c % WQ_RING], 16 * (c // WQ_RING + 1))
                nc.scalar.copy(wq_h[:, c, :], wq_raw[c % WQ_RING][:]).then_inc(wq_hi, 1)
                if c == 1:
                    transposed1(0, 0)
                    normalise1(1, 1)
            run_steps(act, 0, 2, NT - 2, NT, step1)

            phase1_done(act)

            def stack_to_sbuf(n, j):
                for s in range(REP + 1):
                    act.wait_ge(stack_ps, 5 * n + s + 1)
                    dst = k_t[j][0:ST, :] if s == 0 else q_t[j][0:ST, s - 1, :]
                    nc.scalar.copy(dst, bank[s % 2][0:ST, :]).then_inc(stack_sb, 1)

            def shift_to_stack(n, j):
                act.wait_ge(shift_ps, n + 1)
                for h in range(REP):
                    nc.scalar.copy(q_t[j][ST:P, h, :], bank[1][HD * h:HD * h + HD, :]).then_inc(shift_sb, 1)

            def exps(n, j):
                wait(act, pv_ps, n - 1)
                for i in range(3 * REP):
                    h, part = i // 3, i % 3
                    lo, w = ((0, 512), (512, 384), (896, 512))[part]
                    act.wait_ge(score_ps, 12 * n + i + 1)
                    nc.scalar.activation(prob[j][:, h, lo:lo + w], bank[4 + i % 2][:, 0:w], ACT.Exp,
                                         scale=INV_SQRT_HD).then_inc(prob_ready, 1)

            def step2(n, j):
                if live(n + 1, 0, NG):
                    stack_to_sbuf(n + 1, 1 - j)
                if live(n, 0, NG):
                    shift_to_stack(n, j)
                    exps(n, j)

            act.wait_ge(const_ready, 10)
            run_steps(act, -1, 2, NG - 2, NG, step2)

            phase2_done(act)

            def split_att(t):
                act.wait_ge(att_loaded, 16 * t + 16)
                wait(act, o_ps, 2 * t)
                nc.scalar.copy(at_h[:], att_in[:]).then_inc(at_hi, 1)

            def normalise_y(t, j):
                act.wait_ge(y_scale, 8 * t + 4)
                nc.scalar.activation(y[:], y[:], ACT.Identity, bias=ln_nm[0][:], scale=ln_rs[0][:]
                                     ).then_inc(y_norm, 1)
                act.wait_ge(y_scale, 8 * t + 8)
                nc.scalar.activation(y[:], x1[j][:], ACT.Identity, bias=ln_nm[0][:], scale=ln_rs[0][:]
                                     ).then_inc(y_norm, 1)

            def transposed2(t):
                act.wait_ge(xt2_ps, t + 1)
                for h in range(2):
                    last = nc.scalar.copy(xt2_h[:, 4 * h:4 * h + 4, :].rearrange("p c t -> p (c t)"), bank[2 + h][:])
                last.then_inc(xt2_hi, 1)

            def gate(t):
                act.wait_ge(gate_step, 12 * t + 2)
                nc.scalar.activation(gate_e[:], logit[:], ACT.Exp, bias=neg_top[:]).then_inc(gate_exp, 1)

            def low_to_sbuf(t):
                act.wait_ge(low_ps, t + 1)
                nc.scalar.copy(low_h[:], bank[7][:, 0:P]).then_inc(low_hi, 1)

            def normalise_z(t, j):
                act.wait_ge(z_scale, 4 * t + 4)
                nc.scalar.activation(z[j][:], z[j][:], ACT.Identity, bias=ln_nm[1][:], scale=ln_rs[1][:]
                                     ).then_inc(z_norm, 1)

            def step3(t, j):
                if live(t, 0, NT):
                    transposed2(t)
                if live(t - 1, 0, NT):
                    normalise_z(t - 1, 1 - j)
                if live(t + 1, 0, NT):
                    normalise_y(t + 1, 1 - j)
                if live(t + 2, 0, NT):
                    split_att(t + 2)
                if live(t, 0, NT):
                    gate(t)
                    low_to_sbuf(t)

            split_att(0)
            for c in range(KC):
                act.wait_ge(wf_loaded[c % 2], 16 * (c // 2 + 1))
                nc.scalar.copy(wf_h[:, c, :], raw_f[c % 2][:]).then_inc(wf_hi, 1)
            normalise_y(0, 0)
            split_att(1)
            run_steps(act, 0, 2, NT - 2, NT + 1, step3)

        @block.vector
        def _(dve):
            def statistics(src, j, count, before_it):
                for h in range(2):
                    nc.vector.bn_stats(ln_st[j][:, h, :], src[:, HALF * h:HALF * h + HALF]).then_inc(count, 1)
                wait_apart(dve, count, before_it + 2, FIRST_X)
                nc.vector.bn_aggr(ln_mv[j][:], ln_st[j][:]).then_inc(count, 1)

            def stats1(t, j):
                dve.wait_ge(x_loaded[j], 16 * (t // 2) + 16)
                wait(dve, xn_ready, t - 1)
                statistics(x_in[j], j, ln1_step, 3 * t)

            def lo1(t, j):
                dve.wait_ge(xt_hi, t + 1)
                for h in range(2):
                    part = slice(4 * h, 4 * h + 4)
                    last = nc.vector.tensor_tensor(
                        xt_l[j][:, part, :].rearrange("p c t -> p (c t)"), bank[h][:],
                        xt_h[j][:, part, :].rearrange("p c t -> p (c t)").bitcast(F32), ALU.subtract)
                last.then_inc(xt_ready, 1)

            def bias_and_rope(t, j):
                wait(dve, qkv_stored[j], 16 * (t // 2))
                flat = qkv[j][:].rearrange("p g c -> p (g c)")
                for n in range(3):
                    dve.wait_ge(proj_ps, 3 * t + n + 1)
                    cols = slice(HALF * n, HALF * n + HALF)
                    nc.vector.tensor_tensor(flat[:, cols], bank[2 + 3 * j + n][:], bq_row[:, cols], ALU.add
                                            ).then_inc(qkv_step, 1)
                qk = qkv[j][:, :, 0:QKW].rearrange("p g (h c) -> p g h c", c=HD)
                half = HD // 2
                tt = t % TT

                def table(tab, lo, hi):
                    row = tab[:, bass.ds(tt, 1), lo:hi]
                    return row.unsqueeze(1).broadcast_to([P, KV, REP + 1, hi - lo])

                dve.wait_ge(qkv_step, 7 * t + 3)
                nc.vector.tensor_tensor(rope_c[:], qk, table(cos_sb, 0, HD), ALU.mult).then_inc(qkv_step, 1)
                nc.vector.tensor_tensor(rope_s[:, :, :, 0:half], qk[:, :, :, half:HD], table(sin_sb, 0, half),
                                        ALU.mult).then_inc(qkv_step, 1)
                nc.vector.tensor_tensor(rope_s[:, :, :, half:HD], qk[:, :, :, 0:half], table(sin_sb, half, HD),
                                        ALU.mult).then_inc(qkv_step, 1)
                dve.wait_ge(qkv_step, 7 * t + 6)
                nc.vector.tensor_tensor(qk, rope_c[:], rope_s[:], ALU.add).then_inc(qkv_step, 1)

            def step1(t, j):
                if live(t + 1, 0, NT):
                    lo1(t + 1, 1 - j)
                if live(t + 2, 0, NT):
                    stats1(t + 2, j)
                bias_and_rope(t, j)

            stats1(0, 0)
            for c in range(KC):
                dve.wait_ge(wq_hi, c + 1)
                nc.vector.tensor_tensor(wq_l[:, c, :], wq_raw[c % WQ_RING][:], wq_h[:, c, :].bitcast(F32),
                                        ALU.subtract).then_inc(wq_ready, 1)
                if c == 0:
                    stats1(1, 1)
                if c == 2:
                    lo1(0, 0)
            dve.wait_ge(row_loaded, 16 * N_ROWS)
            nc.vector.tensor_copy(ident_r[:], ident[:]).then_inc(const_ready, 1)
            nc.vector.tensor_copy(ident_b[:], ident[:]).then_inc(const_ready, 1)
            nc.vector.tensor_copy(causal_b[:], causal[:]).then_inc(const_ready, 1)
            nc.vector.memset(ones[:], 1.0).then_inc(const_ready, 1)
            run_steps(dve, 0, 2, NT - 2, NT, step1)

            phase1_done(dve)
            for j in range(2):
                nc.vector.memset(k_t[j][ST:P, :].bitcast(F32), 1.0).then_inc(const_ready, 1)
                nc.vector.memset(q_t[j][ST:P, :, :].bitcast(F32), 0.0).then_inc(const_ready, 1)
            nc.vector.memset(shift[:].bitcast(F32), 0.0).then_inc(const_ready, 1)
            nc.vector.memset(neg_max[:], 0.0).then_inc(const_ready, 1)
            dve.wait_ge(const_ready, 10)

            def split(n, j):
                dve.wait_ge(grp_loaded[j], 16 * (n // 2) + 16)
                wait(dve, stack_ps, 5 * (n - 1))
                qk = grp[j][:, :, 0:QKW].rearrange("p t (h c) -> p t h c", c=HD)
                q, k = qk[:, :, 0:REP, :], qk[:, :, REP, :]

                def slot(i):
                    return stack[j][:, :, :, HD * i:HD * i + HD]

                nc.vector.tensor_copy(slot(0), qk).then_inc(split_hi, 1)
                nc.vector.tensor_copy(slot(2)[:, :, 0:REP, :], q).then_inc(split_hi, 1)
                nc.vector.tensor_copy(slot(1)[:, :, REP, :], k).then_inc(split_hi, 1)

            def maxima(n, i0, i1):
                if i0 == 0:
                    wait(dve, shift_step, 2 * n)
                for i in range(i0, i1):
                    h, qb = i // TT, i % TT
                    dve.wait_ge(row_ps, 16 * n + i + 1)
                    nc.vector.tensor_reduce(neg_max[:, qb, h:h + 1], bank[2 + i % 2][:, 0:P * (qb + 1)], AX_X,
                                            ALU.max, negate=True).then_inc(row_max, 1)

            def split_maxima(n):
                wait(dve, shift_ps, n)
                dve.wait_ge(row_max, 16 * n + 16)
                nc.vector.tensor_copy(shift[:, :, :, 0], neg_max[:]).then_inc(shift_step, 1)
                dve.wait_ge(shift_step, 2 * n + 1)
                nc.vector.tensor_tensor(shift[:, :, :, 1], neg_max[:], shift[:, :, :, 0].bitcast(F32),
                                        ALU.subtract).then_inc(shift_step, 1)

            def turn_denominators(n):
                dve.wait_ge(den_ps, n + 1)
                nc.vector.transpose(den_t[:], bank[7][:]).then_inc(den_step, 1)

            def invert_denominators(n):
                dve.wait_ge(den_step, 3 * n + 1)
                nc.vector.reciprocal(den_r[:], den_t[:, 0:SEQ:HD]).then_inc(den_step, 1)

            def spread_inverses(n):
                dve.wait_ge(den_step, 3 * n + 2)
                nc.vector.transpose(den_i[:].rearrange("p (b c) -> p b c", c=HD),
                                    den_r[:].unsqueeze(2).broadcast_to([P, SEQ // HD, HD])).then_inc(den_step, 1)

            def quotient(n, j):
                dve.wait_ge(den_step, 3 * n + 3)
                dve.wait_ge(pv_ps, n + 1)
                wait(dve, att_stored[j], 16 * (n // 2))
                nc.vector.tensor_tensor(att[j][:], bank[6][:], den_i[:], ALU.mult).then_inc(att_ready, 1)

            def step2(n, j):
                after, before_it = live(n + 1, 0, NG), live(n - 1, 0, NG)
                if live(n + 2, 0, NG):
                    split(n + 2, j)
                if after:
                    maxima(n + 1, 0, 4)
                if before_it:
                    turn_denominators(n - 1)
                if after:
                    maxima(n + 1, 4, 6)
                if before_it:
                    invert_denominators(n - 1)
                if after:
                    maxima(n + 1, 6, 8)
                if before_it:
                    spread_inverses(n - 1)
                if after:
                    maxima(n + 1, 8, 10)
                if before_it:
                    quotient(n - 1, 1 - j)
                if after:
                    maxima(n + 1, 10, 16)
                    split_maxima(n + 1)

            split(0, 0)
            run_steps(dve, -1, 4, NG - 2, NG + 1, step2)

            phase2_done(dve)

            def split_att(t):
                dve.wait_ge(at_hi, t + 1)
                nc.vector.tensor_tensor(at_l[:], att_in[:], at_h[:].bitcast(F32), ALU.subtract).then_inc(at_ready, 1)

            def residual1(t, j):
                s = 9 * t
                wait(dve, xt2_ps, t)
                for n in range(2):
                    dve.wait_ge(o_ps, 2 * t + n + 1)
                    cols = slice(HALF * n, HALF * n + HALF)
                    nc.vector.tensor_tensor(y[:, cols], bank[n][:], bo_row[:, cols], ALU.add).then_inc(y_step, 1)
                dve.wait_ge(y_step, s + 2)
                statistics(y, 0, y_step, s + 2)
                dve.wait_ge(res_loaded, 16 * t + 16)
                dve.wait_ge(y_norm, 2 * t + 1)
                nc.vector.tensor_tensor(x1[j][:], y[:], x_res[:], ALU.add).then_inc(y_step, 1)
                dve.wait_ge(y_step, s + 6)
                statistics(x1[j], 0, y_step, s + 6)

            def lo2(t):
                dve.wait_ge(xt2_hi, t + 1)
                for h in range(2):
                    part = slice(4 * h, 4 * h + 4)
                    last = nc.vector.tensor_tensor(
                        xt2_l[:, part, :].rearrange("p c t -> p (c t)"), bank[2 + h][:],
                        xt2_h[:, part, :].rearrange("p c t -> p (c t)").bitcast(F32), ALU.subtract)
                last.then_inc(xt2_ready, 1)

            def gate(t):
                s = 12 * t

                def step(ins):
                    ins.then_inc(gate_step, 1)

                dve.wait_ge(ffn_ps, 3 * t + 1)
                step(nc.vector.tensor_copy(logit[:], bank[4][:, 0:EXP]))
                dve.wait_ge(gate_step, s + 1)
                mine = logit[:].unsqueeze(2).broadcast_to([P, EXP, EXP])
                other = logit[:].unsqueeze(1).broadcast_to([P, EXP, EXP])
                step(nc.vector.tensor_reduce(neg_top[:], logit[:], AX_X, ALU.max, negate=True))
                step(nc.vector.tensor_tensor(equal[:], other, mine, ALU.is_equal))
                step(nc.vector.tensor_tensor(later[:], other, mine, ALU.is_gt))
                dve.wait_ge(gate_step, s + 4)
                step(nc.vector.tensor_tensor(equal[:], equal[:], before[:], ALU.mult))
                dve.wait_ge(gate_step, s + 5)
                step(nc.vector.tensor_tensor(later[:], later[:], equal[:], ALU.add))
                dve.wait_ge(gate_step, s + 6)
                step(nc.vector.tensor_reduce(rank[:], later[:], AX_X, ALU.add))
                dve.wait_ge(gate_step, s + 7)
                dve.wait_ge(gate_exp, t + 1)
                step(nc.vector.scalar_tensor_tensor(out=gate_w[:], in0=rank[:], scalar=1.5, in1=gate_e[:],
                                                    op0=ALU.is_lt, op1=ALU.mult))
                dve.wait_ge(gate_step, s + 8)
                step(nc.vector.tensor_reduce(gate_s[:], gate_w[:], AX_X, ALU.add))
                dve.wait_ge(gate_step, s + 9)
                step(nc.vector.reciprocal(gate_r[:], gate_s[:]))
                dve.wait_ge(gate_step, s + 10)
                step(nc.vector.tensor_scalar(gate_w[:], gate_w[:], gate_r[:], SCALING, ALU.mult, ALU.mult))
                dve.wait_ge(gate_step, s + 11)
                wait(dve, low_ps, t)
                step(nc.vector.tensor_tensor(low[:], bank[4][:, EXP:AGW].rearrange("p (e r) -> p e r", r=RANK),
                                             gate_w[:].unsqueeze(2).broadcast_to([P, EXP, RANK]), ALU.mult))

            def low_lo(t):
                dve.wait_ge(low_hi, t + 1)
                nc.vector.tensor_tensor(low_l[:], bank[7][:, 0:P], low_h[:].bitcast(F32), ALU.subtract
                                        ).then_inc(low_ready, 1)

            def residual2(t, j):
                s = 7 * t
                dve.wait_ge(lora_ps, t + 1)
                wait(dve, out_stored[j], 16 * (t // 2))
                for b, (at, w) in enumerate(FFN_COLS):
                    lo = max(at, AGW)
                    cols = slice(lo - AGW, at + w - AGW)
                    nc.vector.tensor_tensor(z[j][:, cols], bank[4 + b][:, lo - at:w], bf_row[:, cols], ALU.add
                                            ).then_inc(z_step, 1)
                dve.wait_ge(z_step, s + 3)
                statistics(z[j], 1, z_step, s + 3)
                dve.wait_ge(z_norm, t + 1)
                nc.vector.tensor_tensor(z[j][:], z[j][:], x1[j][:], ALU.add).then_inc(z_step, 1)

            def step3(t, j):
                if live(t, 0, NT):
                    lo2(t)
                if live(t - 1, 0, NT):
                    residual2(t - 1, 1 - j)
                if live(t + 1, 0, NT):
                    residual1(t + 1, 1 - j)
                if live(t + 2, 0, NT):
                    split_att(t + 2)
                if live(t, 0, NT):
                    gate(t)
                    low_lo(t)

            split_att(0)
            for c in range(KC):
                dve.wait_ge(wf_hi, c + 1)
                nc.vector.tensor_tensor(wf_l[:, c, :], raw_f[c % 2][:], wf_h[:, c, :].bitcast(F32), ALU.subtract
                                        ).then_inc(wf_ready, 1)
            residual1(0, 0)
            split_att(1)
            run_steps(dve, 0, 4, NT - 2, NT + 1, step3)

        @block.tensor
        def _(pe):
            mm = nc.tensor.matmul

            def product(dst, a_h, a_l, w_h, w_l, start, stop):
                mm(dst, a_h, w_h, start=start, stop=False, skip_group_check=True)
                mm(dst, a_l, w_h, start=False, stop=False, skip_group_check=True)
                return mm(dst, a_h, w_l, start=False, stop=stop, skip_group_check=True)

            def transpose1(t, j):
                pe.wait_ge(xn_ready, t + 1)
                wait(pe, xt_ready, t)
                for c in range(KC):
                    last = nc.tensor.transpose(bank[c // 4][:, P * (c % 4):P * (c % 4) + P],
                                               xn[j][:, P * c:P * c + P], ident[:])
                last.then_inc(xt_ps, 1)

            def project(t, j):
                pe.wait_ge(xt_ready, t + 1)
                for n in range(3):
                    wait(pe, qkv_step, 7 * (t - 2) + n + 1)
                    cols = slice(HALF * n, HALF * n + HALF)
                    for c in range(KC):
                        if isinstance(t, int) and t == 0 and n == 0:
                            pe.wait_ge(wq_ready, c + 1)
                        last = product(bank[2 + 3 * j + n][:], xt_h[j][:, c, :], xt_l[j][:, c, :],
                                       wq_h[:, c, cols], wq_l[:, c, cols], c == 0, c == KC - 1)
                    last.then_inc(proj_ps, 1)

            def step1(t, j):
                if live(t + 1, 0, NT):
                    transpose1(t + 1, 1 - j)
                project(t, j)

            pe.wait_ge(row_loaded, 16 * N_ROWS)
            transpose1(0, 0)
            run_steps(pe, 0, 2, NT - 2, NT, step1)

            phase1_done(pe)
            pe.wait_ge(const_ready, 10)

            def stack_transpose(n, j, s):
                if s == 0:
                    pe.wait_ge(split_hi, 3 * n + 3)
                    pe.wait_ge(split_lo, 2 * n + 2)
                    wait(pe, stack_sb, 5 * n)
                elif s == 1:
                    wait(pe, shift_sb, 4 * (n - 1))
                else:
                    pe.wait_ge(stack_sb, 5 * n + s - 1)
                head = REP if s == 0 else s - 1
                for tt in range(TT):
                    last = nc.tensor.transpose(bank[s % 2][0:ST, P * tt:P * tt + P].bitcast(F32R),
                                               stack[j][:, tt, head, :], ident_r[:])
                last.then_inc(stack_ps, 1)

            def shift_transpose(n):
                pe.wait_ge(shift_step, 2 * n + 2)
                wait(pe, shift_sb, 4 * n)
                wait(pe, stack_sb, 5 * min(n + 1, NG - 1) + 4 if isinstance(n, int) else 5 * n + 9)
                for tt in range(TT):
                    last = nc.tensor.transpose(bank[1][:, P * tt:P * tt + P].bitcast(F32R),
                                               shift[:, tt, :, :].rearrange("p h c -> p (h c)"), ident_r[:])
                last.then_inc(shift_ps, 1)

            def row_scores(n, j, i):
                h, qb = i // TT, i % TT
                if qb == 0:
                    pe.wait_ge(stack_sb, 5 * n + 2 + h)
                wait(pe, row_max, 16 * n + i - 1)
                w = max(P * (qb + 1), 2 * P)
                diag = slice(P * qb, P * qb + P)
                mm(bank[2 + i % 2][:, 0:w], q_t[j][0:ST, h, diag], k_t[j][0:ST, 0:w], start=True, stop=False,
                   skip_group_check=True)
                mm(bank[2 + i % 2][:, diag], ident_b[:], causal_b[:], start=False, stop=True,
                   skip_group_check=True).then_inc(row_ps, 1)

            def scores(n, j, i):
                h, part = i // 3, i % 3
                if part == 0:
                    pe.wait_ge(shift_sb, 4 * n + h + 1)
                wait(pe, prob_ready, 12 * n + i - 1)
                for kc, at, q0 in (((0, 0, 0),), ((1, 0, P),), ((2, 0, 2 * P), (3, 2 * P, 2 * P)))[part]:
                    w = SEQ - q0
                    last = mm(bank[4 + i % 2][:, at:at + w], k_t[j][:, P * kc:P * kc + P], q_t[j][:, h, q0:SEQ],
                              start=True, stop=True, skip_group_check=True)
                last.then_inc(score_ps, 1)

            def weigh(n, j, kc, values):
                if kc == 0:
                    if values:
                        wait(pe, att_ready, n)
                        pe.wait_ge(v_loaded[j], 16 * (n // 2) + 16)
                    else:
                        pe.wait_ge(prob_masked, 8 * n + 8)
                        wait(pe, den_step, 3 * n - 2)
                at = (0, 512, 896, 1280)[kc]
                w = SEQ - P * kc
                dst = bank[6] if values else bank[7]
                for h in range(REP):
                    last = mm(dst[HD * h:HD * h + HD, P * kc:SEQ], v_sb[j][:, kc, :] if values else ones[:],
                              prob[j][:, h, at:at + w], start=(kc == 0), stop=(kc == TT - 1), skip_group_check=True)
                if kc == TT - 1:
                    last.then_inc(pv_ps if values else den_ps, 1)

            def step2(n, j):
                before_it, after = live(n - 1, 0, NG), live(n + 1, 0, NG)
                for s in range(REP + 1):
                    if after:
                        stack_transpose(n + 1, 1 - j, s)
                    if before_it and s >= 1:
                        weigh(n - 1, 1 - j, s - 1, False)
                if live(n, 0, NG):
                    shift_transpose(n)
                for i in range(16):
                    if before_it and i < 4:
                        weigh(n - 1, 1 - j, i, True)
                    if after:
                        row_scores(n + 1, 1 - j, i)
                    if live(n, 0, NG) and i % 4 < 3:
                        scores(n, j, 3 * (i // 4) + i % 4)

            run_steps(pe, -1, 2, NG - 2, NG + 1, step2)

            phase2_done(pe)

            def project_out(t):
                pe.wait_ge(at_ready, t + 1)
                for n in range(2):
                    wait(pe, y_step, 9 * (t - 1) + n + 1)
                    for c in range(KC):
                        cols = slice(D * c + HALF * n, D * c + HALF * n + HALF)
                        last = product(bank[n][:], at_h[:, c, :], at_l[:, c, :], wo_h[:, cols], wo_l[:, cols],
                                       c == 0, c == KC - 1)
                    last.then_inc(o_ps, 1)

            def transpose2(t):
                pe.wait_ge(y_norm, 2 * t + 2)
                wait(pe, xt2_ready, t)
                for c in range(KC):
                    last = nc.tensor.transpose(bank[2 + c // 4][:, P * (c % 4):P * (c % 4) + P],
                                               y[:, P * c:P * c + P], ident[:])
                last.then_inc(xt2_ps, 1)

            def ffn(t):
                pe.wait_ge(xt2_ready, t + 1)
                wait(pe, z_step, 7 * (t - 1) + 3)
                for b, (at, w) in enumerate(FFN_COLS):
                    for c in range(KC):
                        if isinstance(t, int) and t == 0 and b == 0:
                            pe.wait_ge(wf_ready, c + 1)
                        last = product(bank[4 + b][:, 0:w], xt2_h[:, c, :], xt2_l[:, c, :], wf_h[:, c, at:at + w],
                                       wf_l[:, c, at:at + w], c == 0, False)
                    last.then_inc(ffn_ps, 1)
                pe.wait_ge(gate_step, 12 * t + 12)
                wait(pe, low_ready, t)
                nc.tensor.transpose(bank[7][:, 0:P], low[:].rearrange("p e r -> p (e r)"), ident[:]).then_inc(low_ps, 1)

            def lora(t):
                pe.wait_ge(low_ready, t + 1)
                for b, (at, w) in enumerate(FFN_COLS):
                    lo = max(at, AGW)
                    cols = slice(KC * D + lo - AGW, KC * D + at + w - AGW)
                    last = product(bank[4 + b][:, lo - at:w], low_h[:], low_l[:], wo_h[:, cols], wo_l[:, cols],
                                   False, True)
                last.then_inc(lora_ps, 1)

            def step3(t, j):
                if live(t, 0, NT):
                    transpose2(t)
                if live(t - 1, 0, NT):
                    lora(t - 1)
                if live(t + 1, 0, NT):
                    project_out(t + 1)
                if live(t, 0, NT):
                    ffn(t)

            project_out(0)
            run_steps(pe, 0, 2, NT - 2, NT + 1, step3)


def kernel(L0_attn_x, L0_attn_w_qkv, L0_attn_b_qkv, L0_attn_w_o, L0_attn_b_o, L0_ffn_gate_w, L0_ffn_base_w,
           L0_ffn_base_b, L0_ffn_lora_A, L0_ffn_lora_B):
    import numpy as np
    import concourse.bacc as bacc
    from concourse import mybir as mb
    from concourse.bass_utils import run_bass_kernel_spmd

    halves = np.concatenate([np.arange(0, HD, 2), np.arange(1, HD, 2)])
    order = []
    for g in range(KV):
        for h in range(REP):
            order.append((REP * g + h) * HD + halves)
        order.append(HEADS * HD + g * HD + halves)
        order.append((HEADS + KV) * HD + g * HD + np.arange(HD))
    order = np.concatenate(order)

    def by_partition(w_t):
        return np.ascontiguousarray(w_t.reshape(KC, P, -1).transpose(1, 0, 2))

    arr = {k: np.asarray(v) for k, v in locals().items() if k.startswith("L0_")}
    w_qkv = by_partition(arr["L0_attn_w_qkv"][order].T)
    w_o = by_partition(arr["L0_attn_w_o"].T).reshape(P, KC * D)
    lora_b = arr["L0_ffn_lora_B"].transpose(0, 2, 1).reshape(ER, D)
    w_ffn = np.concatenate([arr["L0_ffn_gate_w"].T, arr["L0_ffn_lora_A"].reshape(ER, D).T, arr["L0_ffn_base_w"].T], 1)

    inv = np.float32(1.0) / np.float32(10000.0) ** (np.arange(0, HD, 2, dtype=np.float32) / np.float32(HD))
    ang = np.arange(SEQ, dtype=np.float32)[:, None] * inv[None, :].astype(np.float32)
    cos, sin = np.cos(ang).astype(np.float32), np.sin(ang).astype(np.float32)

    def table(t):
        return np.ascontiguousarray(t.reshape(TT, P, HD).transpose(1, 0, 2))

    inputs = {
        "x": np.ascontiguousarray(arr["L0_attn_x"].reshape(NT, P, D)),
        "w_qkv": w_qkv,
        "b_qkv": np.ascontiguousarray(arr["L0_attn_b_qkv"][order][None]),
        "w_out": np.ascontiguousarray(np.concatenate([w_o, lora_b], 1)),
        "b_o": np.ascontiguousarray(arr["L0_attn_b_o"][None]),
        "w_ffn": by_partition(w_ffn),
        "b_ffn": np.ascontiguousarray(arr["L0_ffn_base_b"][None]),
        "cos_t": table(np.concatenate([cos, cos], 1)),
        "sin_t": table(np.concatenate([-sin, sin], 1)),
        "ident": np.eye(P, dtype=np.float32),
        "causal": np.where(np.tril(np.ones((P, P), bool)), 0.0, MASKED).astype(np.float32),
        "before": np.tril(np.ones((EXP, EXP), np.float32), -1)[None],
    }
    nc = bacc.Bacc("TRN2", target_bir_lowering=False, num_devices=1)
    aps = [nc.dram_tensor(k, v.shape, mb.dt.from_np(v.dtype), kind="ExternalInput").ap() for k, v in inputs.items()]
    out = nc.dram_tensor("out", (NT, P, D), mb.dt.float32, kind="ExternalOutput").ap()
    build(nc, *aps, out)
    result = run_bass_kernel_spmd(nc, [inputs], core_ids=[0])
    return result.results[0]["out"].reshape(BATCH, SEQ, D)
```

```python
from contextlib import ExitStack

import concourse.bass as bass
from concourse import mybir

F32 = mybir.dt.float32
F32R = mybir.dt.float32r
BF16 = mybir.dt.bfloat16
ALU = mybir.AluOpType
ACT = mybir.ActivationFunctionType
AX_X = mybir.AxisListType.X

P = 128
D = 1024
KC = D // P
BATCH, SEQ = 4, 512
NT = BATCH * SEQ // P
TT = SEQ // P
HEADS, KV, HD = 32, 8, 32
REP = HEADS // KV
GW = (REP + 2) * HD
QKW = (REP + 1) * HD
QKV = KV * GW
NG = BATCH * KV
EXP, RANK = 8, 16
ER = EXP * RANK
AGW = EXP + ER
FW = AGW + D
EPS = 1e-5
SCALING = 2.0
INV_SQRT_HD = float(HD) ** -0.5
HALF = 512
MASKED = -1.0e30
STACKS = (0, REP, 1, 2, 3)
ST = 3 * HD
OUT_SPLIT = (KC + 1) * D
PIECE = OUT_SPLIT // NG
FFN_COLS = [(0, AGW + 256), (AGW + 256, 384), (AGW + 640, 384)]
WQ_RING = 4
WF_RING = 4
UNITS = 3 * REP


def wait(eng, sem, value):
    if not (isinstance(value, int) and value <= 0):
        eng.wait_ge(sem, value)


def wait_apart(eng, sem, value, passed):
    if not (isinstance(value, int) and value <= 0):
        if not isinstance(value, int):
            eng.compute_val(value)
            eng.wait_ge(*passed)
        eng.wait_ge(sem, value)


def live(n, lo, hi):
    return not isinstance(n, int) or lo <= n < hi


def run_steps(eng, first, lo, hi, last, step):
    for n in range(first, lo):
        step(n, n % 2)
    with eng.Fori(lo // 2, hi // 2) as i:
        for j in range(2):
            step(2 * i + j, j)
    for n in range(hi, last):
        step(n, n % 2)


def build(nc, x, w_qkv, b_qkv, w_out, b_o, w_ffn, b_ffn, cos_t, sin_t, ident_h, causal_h, before_h, out):
    qkv_scratch = nc.dram_tensor("qkv_scratch", [NT, P, QKV], F32).ap()
    att_scratch = nc.dram_tensor("att_scratch", [NG // KV, KV, P, SEQ], F32).ap()

    with ExitStack() as ctx:
        arena = ctx.enter_context(nc.sbuf_tensor("arena", [P, 212000], mybir.dt.uint8))
        del arena
        start = 16640
        limit = 16512 + 212000

        def sem(name):
            return ctx.enter_context(nc.semaphore(name))

        class Map:

            def __init__(self, at):
                self.at = at

            def __call__(self, name, shape, dtype=F32):
                size = mybir.dt.size(dtype)
                for n in shape[1:]:
                    size *= n
                t = nc.alloc_sbuf_tensor_at(name, shape, dtype, offset=self.at)
                self.at += -(-size // 32) * 32
                assert self.at <= limit, (name, self.at - limit)
                return t

        m = Map(start)
        ident = m("ident", [P, P])
        ident_r = m("ident_r", [P, P], F32R)
        ident_b = m("ident_b", [P, P], BF16)
        causal_b = m("causal_b", [P, P], BF16)
        causal = m("causal", [P, P])
        ones = m("ones", [P, HD])
        before = m("before", [P, EXP, EXP])
        bo_row = m("bo_row", [P, D])
        bf_row = m("bf_row", [P, D])
        ln_st = [m(f"ln_st{j}", [P, 2, 6]) for j in range(2)]
        ln_mv = [m(f"ln_mv{j}", [P, 2]) for j in range(2)]
        ln_rs = [m(f"ln_rs{j}", [P, 1]) for j in range(2)]
        ln_nm = [m(f"ln_nm{j}", [P, 1]) for j in range(2)]
        ln_ve = [m(f"ln_ve{j}", [P, 1]) for j in range(2)]
        ln_mm = [m(f"ln_mm{j}", [P, 1]) for j in range(2)]
        minus_half = m("minus_half", [P, 1])
        minus_one = m("minus_one", [P, 1])
        eps_col = m("eps_col", [P, 1])
        common_end = m.at

        phase1_at = common_end
        m = Map(phase1_at)
        wq_h = m("wq_h", [P, KC, QKV], F32R)
        wq_l = m("wq_l", [P, KC, QKV], F32R)
        wq_raw = [m(f"wq_raw{j}", [P, QKV]) for j in range(WQ_RING)]
        wq_end = m.at

        m = Map(phase1_at)
        wo_h = m("wo_h", [P, OUT_SPLIT], F32R)
        wo_l = m("wo_l", [P, OUT_SPLIT], F32R)
        phase3_at = m.at
        q_t = [m(f"q_t{j}", [P, REP, SEQ], F32R) for j in range(2)]
        shift = m("shift", [P, TT, REP, HD], F32R)
        neg_max = m("neg_max", [P, TT, REP])
        den_r = m("den_r", [P, SEQ // HD])
        z_at = m.at
        den_t = m("den_t", [P, SEQ])
        den_i = m("den_i", [P, SEQ])
        att = [m(f"att{j}", [P, SEQ]) for j in range(2)]
        raw_at = m.at
        grp = [m(f"grp{j}", [P, TT, GW]) for j in range(2)]
        stack = [m(f"stack{j}", [P, TT, REP + 1, ST], F32R) for j in range(2)]
        raw_limit = m.at
        v_sb = [m(f"v_sb{j}", [P, TT, HD]) for j in range(2)]
        wo_raw = [m(f"wo_raw{j}", [P, PIECE]) for j in range(2)]
        k_t = [m(f"k_t{j}", [P, SEQ], F32R) for j in range(2)]
        assert m.at >= wq_end
        prob_at = m.at
        prob = [m(f"prob{j}", [P, REP, 1408]) for j in range(2)]
        phase2_end = m.at

        m = Map(prob_at)
        x_in = [m(f"x_in{j}", [P, D]) for j in range(2)]
        xn = [m(f"xn{j}", [P, D]) for j in range(2)]
        xt_h = [m(f"xt_h{j}", [P, KC, P], F32R) for j in range(2)]
        xt_l = [m(f"xt_l{j}", [P, KC, P], F32R) for j in range(2)]
        qkv = [m(f"qkv{j}", [P, KV, GW]) for j in range(2)]
        qkv_end = m.at

        m = Map(phase3_at)
        x1 = [m(f"x1_{j}", [P, D]) for j in range(2)]
        y = m("y", [P, D])
        wf_h, wf_l = [None] * KC, [None] * KC
        wf_h[0] = m("wf_h0", [P, FW], F32R)
        assert m.at <= z_at
        m = Map(z_at)
        z = [m(f"z{j}", [P, D]) for j in range(2)]
        assert m.at <= raw_at
        m = Map(raw_at)
        raw_f = [m(f"raw_f{j}", [P, FW]) for j in range(WF_RING)]
        assert m.at <= raw_limit
        m = Map(raw_at)
        xt2_h = m("xt2_h", [P, KC, P], F32R)
        xt2_l = m("xt2_l", [P, KC, P], F32R)
        low_h = m("low_h", [P, P], F32R)
        low_l = m("low_l", [P, P], F32R)
        m = Map(raw_at + 2 * FW * 4)
        wf_l[KC - 2] = m(f"wf_l{KC - 2}", [P, FW], F32R)
        wf_l[KC - 1] = m(f"wf_l{KC - 1}", [P, FW], F32R)
        for c in range(1, KC):
            wf_h[c] = m(f"wf_h{c}", [P, FW], F32R)
        for c in range(1, KC - 2):
            wf_l[c] = m(f"wf_l{c}", [P, FW], F32R)
        m = Map(max(m.at, phase2_end, qkv_end))
        tables_at = m.at
        at_in = m("at_in", [P, KC, P])
        at_h = m("at_h", [P, KC, P], F32R)
        at_l = m("at_l", [P, KC, P], F32R)
        x_res = m("x_res", [P, D])
        wf_l[0] = m("wf_l0", [P, FW], F32R)
        low = m("low", [P, EXP, RANK])
        logit = m("logit", [P, EXP])
        later = m("later", [P, EXP, EXP])
        equal = m("equal", [P, EXP, EXP])
        rank = m("rank", [P, EXP])
        neg_top = m("neg_top", [P, 1])
        gate_e = m("gate_e", [P, EXP])
        gate_w = m("gate_w", [P, EXP])
        gate_s = m("gate_s", [P, 1])
        gate_r = m("gate_r", [P, 1])

        m = Map(tables_at)
        rope_c = m("rope_c", [P, KV, REP + 1, HD])
        rope_s = m("rope_s", [P, KV, REP + 1, HD])
        bq_row = m("bq_row", [P, QKV])
        cos_sb = m("cos_sb", [P, TT, HD])
        sin_sb = m("sin_sb", [P, TT, HD])

        bank = [ctx.enter_context(nc.psum_tensor(f"bank{i}", [P, HALF], F32)) for i in range(8)]

        ident_loaded = sem("ident_loaded")
        row_loaded = sem("row_loaded")
        late_loaded = sem("late_loaded")
        const_ready = sem("const_ready")
        wq_loaded = [sem(f"wq_loaded{j}") for j in range(WQ_RING)]
        wq_hi = sem("wq_hi")
        wq_ready = sem("wq_ready")
        x_loaded = [sem(f"x_loaded{j}") for j in range(2)]
        ln1_step = sem("ln1_step")
        ln1_norm = sem("ln1_norm")
        half_set = sem("half_set")
        xn_ready = sem("xn_ready")
        xt_ps = sem("xt_ps")
        xt_hi = sem("xt_hi")
        xt_ready = sem("xt_ready")
        proj_ps = sem("proj_ps")
        qkv_step = sem("qkv_step")
        qkv_stored = [sem(f"qkv_stored{j}") for j in range(2)]
        grp_loaded = [sem(f"grp_loaded{j}") for j in range(2)]
        v_loaded = [sem(f"v_loaded{j}") for j in range(2)]
        wo_loaded = [sem(f"wo_loaded{j}") for j in range(2)]
        wo_hi = sem("wo_hi")
        wo_ready = sem("wo_ready")
        split_hi = sem("split_hi")
        split_lo = sem("split_lo")
        stack_ps = sem("stack_ps")
        stack_sb = sem("stack_sb")
        row_ps = sem("row_ps")
        row_max = sem("row_max")
        shift_step = sem("shift_step")
        shift_ps = sem("shift_ps")
        shift_sb = sem("shift_sb")
        score_ps = sem("score_ps")
        prob_ready = sem("prob_ready")
        prob_masked = sem("prob_masked")
        den_ps = sem("den_ps")
        den_step = sem("den_step")
        pv_ps = sem("pv_ps")
        att_ready = sem("att_ready")
        att_stored = [sem(f"att_stored{j}") for j in range(2)]
        wf_loaded = [sem(f"wf_loaded{j}") for j in range(WF_RING)]
        wf_hi = sem("wf_hi")
        wf_ready = sem("wf_ready")
        att_loaded = sem("att_loaded")
        res_loaded = sem("res_loaded")
        at_hi = sem("at_hi")
        at_ready = sem("at_ready")
        o_ps = sem("o_ps")
        y_step = sem("y_step")
        y_scale = sem("y_scale")
        y_norm = sem("y_norm")
        xt2_ps = sem("xt2_ps")
        xt2_hi = sem("xt2_hi")
        xt2_ready = sem("xt2_ready")
        ffn_ps = sem("ffn_ps")
        gate_step = sem("gate_step")
        gate_exp = sem("gate_exp")
        low_ps = sem("low_ps")
        low_hi = sem("low_hi")
        low_ready = sem("low_ready")
        lora_ps = sem("lora_ps")
        z_step = sem("z_step")
        z_scale = sem("z_scale")
        z_norm = sem("z_norm")
        out_stored = [sem(f"out_stored{j}") for j in range(2)]

        block = ctx.enter_context(nc.Block())

        N_ROWS = 4
        N_LATE = 3
        FIRST_X = (x_loaded[0], 16)

        @block.sync
        def _(sp):
            sp.dma_start(x_in[0][:], x[0]).then_inc(x_loaded[0], 16)
            sp.dma_start(ident[:], ident_h).then_inc(ident_loaded, 16)
            sp.dma_start(wq_raw[0][:], w_qkv[:, 0, :]).then_inc(wq_loaded[0], 16)
            sp.dma_start(x_in[1][:], x[1]).then_inc(x_loaded[1], 16)
            for c in range(1, WQ_RING):
                sp.dma_start(wq_raw[c][:], w_qkv[:, c, :]).then_inc(wq_loaded[c], 16)

            def load_x(t, j):
                wait_apart(sp, xn_ready, t - 1, FIRST_X)
                sp.dma_start(x_in[j][:], x[t]).then_inc(x_loaded[j], 16)

            for c in range(WQ_RING, KC):
                if c == KC - 1:
                    load_x(2, 0)
                sp.wait_ge(wq_ready, c - WQ_RING + 1)
                sp.dma_start(wq_raw[c % WQ_RING][:], w_qkv[:, c, :]).then_inc(wq_loaded[c % WQ_RING], 16)
            sp.dma_start(bq_row[:], b_qkv[0].partition_broadcast(P)).then_inc(row_loaded, 16)
            sp.dma_start(cos_sb[:], cos_t).then_inc(row_loaded, 16)
            sp.dma_start(sin_sb[:], sin_t).then_inc(row_loaded, 16)
            sp.dma_start(causal[:], causal_h).then_inc(row_loaded, 16)
            load_x(3, 1)
            sp.dma_start(before[:], before_h[0].partition_broadcast(P)).then_inc(late_loaded, 16)
            sp.dma_start(bo_row[:], b_o[0].partition_broadcast(P)).then_inc(late_loaded, 16)
            sp.dma_start(bf_row[:], b_ffn[0].partition_broadcast(P)).then_inc(late_loaded, 16)

            def store_qkv(t, j):
                wait_apart(sp, qkv_step, 7 * t + 7, FIRST_X)
                sp.dma_start(qkv_scratch[t], qkv[j][:].rearrange("p g c -> p (g c)")).then_inc(qkv_stored[j], 16)

            def io1(t, j):
                if live(t + 2, 4, NT):
                    load_x(t + 2, j)
                store_qkv(t, j)

            def group(n):
                return n // KV, n % KV

            def load_group(n, j):
                b, g = group(n)
                wait_apart(sp, split_hi, 3 * (n - 1), FIRST_X)
                wait(sp, split_lo, 2 * (n - 1))
                if isinstance(n, int):
                    for i in range(2):
                        sp.wait_ge(qkv_stored[i], 16 * TT // 2 * (b + 1))
                src = qkv_scratch.rearrange("(b t) p (g c) -> b g p t c", t=TT, c=GW)[b, g]
                sp.dma_start(grp[j][:], src).then_inc(grp_loaded[j], 16)

            def load_v(n, j):
                b, g = group(n)
                wait_apart(sp, pv_ps, n - 1, FIRST_X)
                src = qkv_scratch.rearrange("(b t) p (g c) -> b g p t c", t=TT, c=GW)[b, g][:, :, QKW:GW]
                sp.dma_start(v_sb[j][:], src).then_inc(v_loaded[j], 16)

            def load_piece(n, j):
                wait_apart(sp, wo_ready, n - 1, FIRST_X)
                src = w_out.rearrange("p (n c) -> n p c", c=PIECE)[n]
                sp.dma_start(wo_raw[j][:], src).then_inc(wo_loaded[j], 16)

            def store_att(n, j):
                b, g = group(n)
                wait_apart(sp, att_ready, n + 1, FIRST_X)
                sp.dma_start(att_scratch[b, g], att[j][:]).then_inc(att_stored[j], 16)

            def io2(n, j):
                if live(n + 3, 2, NG):
                    load_group(n + 3, 1 - j)
                if live(n - 2, 0, NG):
                    store_att(n - 2, j)
                if live(n + 2, 2, NG):
                    load_piece(n + 2, j)
                if live(n + 1, 2, NG):
                    load_v(n + 1, 1 - j)

            run_steps(sp, 0, 2, NT - 2, NT - 2, io1)
            load_piece(0, 0)
            load_piece(1, 1)
            load_group(0, 0)
            load_group(1, 1)
            load_v(0, 0)
            load_v(1, 1)
            io1(NT - 2, 0)
            io2(-1, 1)
            store_qkv(NT - 1, 1)
            for i in range(2):
                sp.wait_ge(qkv_stored[i], 16 * (NT // 2))
            run_steps(sp, 0, 2, NG - 4, NG, io2)

            def load_att(t):
                wait_apart(sp, at_ready, t, FIRST_X)
                for i in range(2):
                    wait(sp, att_stored[i], 16 * KV // 2 * (t // TT + 1))
                src = att_scratch.rearrange("b g p (t c) -> b t p g c", c=P)[t // TT, t % TT]
                sp.dma_start(at_in[:], src).then_inc(att_loaded, 16)

            def load_res(t):
                wait_apart(sp, y_step, 9 * (t - 1) + 6, FIRST_X)
                sp.dma_start(x_res[:], x[t]).then_inc(res_loaded, 16)

            def load_ffn(c):
                wait(sp, wf_ready, c - WF_RING + 1)
                sp.dma_start(raw_f[c % WF_RING][:], w_ffn[:, c, :]).then_inc(wf_loaded[c % WF_RING], 16)

            def store_out(t, j):
                wait_apart(sp, z_step, 7 * t + 7, FIRST_X)
                sp.dma_start(out[t], z[j][:]).then_inc(out_stored[j], 16)

            load_att(0)
            load_res(0)
            sp.wait_ge(stack_ps, 5 * NG)
            sp.wait_ge(split_lo, 2 * NG)
            for c in range(WF_RING):
                load_ffn(c)
            io2(NG, 0)
            io2(NG + 1, 1)
            for c in range(WF_RING, KC):
                load_ffn(c)
            load_att(1)
            load_res(1)

            def io3(t, j):
                if live(t + 2, 0, NT):
                    load_att(t + 2)
                if live(t - 1, 0, NT):
                    store_out(t - 1, 1 - j)
                if live(t + 2, 0, NT):
                    load_res(t + 2)

            run_steps(sp, 0, 2, NT - 2, NT + 1, io3)
            for j in range(2):
                sp.wait_ge(out_stored[j], 16 * (NT // 2))

        @block.gpsimd
        def _(pool):
            def scale_and_shift(j, count, before_it):
                nc.gpsimd.tensor_tensor(ln_ve[j][:], ln_mv[j][:, 1:2], eps_col[:], ALU.add).then_inc(count, 1)
                nc.gpsimd.tensor_tensor(ln_mm[j][:], ln_mv[j][:, 0:1], minus_one[:], ALU.mult).then_inc(count, 1)
                pool.wait_ge(count, before_it + 1)
                nc.gpsimd.tensor_tensor(ln_rs[j][:], ln_ve[j][:], minus_half[:], ALU.pow).then_inc(count, 1)
                pool.wait_ge(count, before_it + 3)
                nc.gpsimd.tensor_tensor(ln_nm[j][:], ln_mm[j][:], ln_rs[j][:], ALU.mult).then_inc(count, 1)

            def scale1(t, j):
                pool.wait_ge(ln1_step, 3 * t + 3)
                scale_and_shift(j, ln1_norm, 4 * t)

            nc.gpsimd.memset(minus_half[:], -0.5).then_inc(half_set, 1)
            nc.gpsimd.memset(minus_one[:], -1.0).then_inc(half_set, 1)
            nc.gpsimd.memset(eps_col[:], EPS).then_inc(half_set, 1)
            pool.wait_ge(half_set, 3)
            run_steps(pool, 0, 2, NT, NT, scale1)

            def mask(n, j, h):
                wait_apart(pool, prob_ready, UNITS * n + 3 * h + 3, (half_set, 3))
                d0 = prob[j][:, h, 0:P]
                nc.gpsimd.affine_select(out=d0, in_=d0, compare_op=ALU.is_ge, fill=0.0, base=0,
                                        pattern=[[1, P]], channel_multiplier=-1).then_inc(prob_masked, 1)
                d1 = prob[j][:, h, 512:1408].rearrange("p (a c) -> p a c", c=P)[:, 0:7:3, :]
                nc.gpsimd.affine_select(out=d1, in_=d1, compare_op=ALU.is_ge, fill=0.0, base=0,
                                        pattern=[[0, 3], [1, P]], channel_multiplier=-1).then_inc(prob_masked, 1)

            def piece_hi(n, j):
                wait_apart(pool, wo_loaded[j], 16 * (n // 2) + 16, (half_set, 3))
                nc.gpsimd.tensor_copy(wo_h[:, bass.ds(n * PIECE, PIECE)], wo_raw[j][:]).then_inc(wo_hi, 1)

            def piece_lo(n, j):
                hi = wo_h[:, bass.ds(n * PIECE, PIECE)]
                lo = wo_l[:, bass.ds(n * PIECE, PIECE)]
                pool.wait_ge(wo_hi, n + 1)
                nc.gpsimd.tensor_tensor(lo, wo_raw[j][:], hi.bitcast(F32), ALU.subtract).then_inc(wo_ready, 1)

            def split_group(n, j):
                pool.wait_ge(split_hi, 3 * n + 3)
                qk = grp[j][:, :, 0:QKW].rearrange("p t (h c) -> p t h c", c=HD)
                hi = stack[j][:, :, :, 0:HD].bitcast(F32)
                nc.gpsimd.tensor_tensor(stack[j][:, :, 0:REP, HD:2 * HD], qk[:, :, 0:REP, :], hi[:, :, 0:REP, :],
                                        ALU.subtract).then_inc(split_lo, 1)
                nc.gpsimd.tensor_tensor(stack[j][:, :, REP, 2 * HD:ST], qk[:, :, REP, :], hi[:, :, REP, :],
                                        ALU.subtract).then_inc(split_lo, 1)

            def step2(n, j):
                if live(n + 2, 0, NG):
                    split_group(n + 2, j)
                mask(n, j, 0)
                mask(n, j, 1)
                piece_hi(n, j)
                mask(n, j, 2)
                piece_lo(n, j)
                mask(n, j, 3)

            split_group(0, 0)
            split_group(1, 1)
            pool.wait_ge(proj_ps, 3 * NT)
            run_steps(pool, 0, 2, NG - 2, NG, step2)

            def scale_y(t):
                pool.wait_ge(y_step, 9 * t + 5)
                wait(pool, y_norm, 2 * t)
                scale_and_shift(0, y_scale, 8 * t)
                pool.wait_ge(y_step, 9 * t + 9)
                scale_and_shift(0, y_scale, 8 * t + 4)

            def scale_z(t):
                pool.wait_ge(z_step, 7 * t + 6)
                scale_and_shift(1, z_scale, 4 * t)

            def step3(t, j):
                if live(t - 1, 0, NT):
                    scale_z(t - 1)
                if live(t + 1, 0, NT):
                    scale_y(t + 1)

            scale_y(0)
            run_steps(pool, 0, 2, NT - 2, NT + 1, step3)

        @block.scalar
        def _(act):
            def normalise1(t, j):
                act.wait_ge(ln1_norm, 4 * t + 4)
                wait(act, xt_ps, t - 1)
                nc.scalar.activation(xn[j][:], x_in[j][:], ACT.Identity, bias=ln_nm[j][:], scale=ln_rs[j][:]
                                     ).then_inc(xn_ready, 1)

            def transposed1(t, j):
                wait(act, proj_ps, 3 * (t - 1))
                act.wait_ge(xt_ps, t + 1)
                for h in range(2):
                    last = nc.scalar.copy(xt_h[j][:, 4 * h:4 * h + 4, :].rearrange("p c t -> p (c t)"), bank[h][:])
                last.then_inc(xt_hi, 1)

            def step1(t, j):
                if live(t + 1, 0, NT):
                    transposed1(t + 1, 1 - j)
                if live(t + 2, 0, NT):
                    normalise1(t + 2, j)

            normalise1(0, 0)
            for c in range(KC):
                act.wait_ge(wq_loaded[c % WQ_RING], 16 * (c // WQ_RING + 1))
                nc.scalar.copy(wq_h[:, c, :], wq_raw[c % WQ_RING][:]).then_inc(wq_hi, 1)
                if c == 0:
                    transposed1(0, 0)
                elif c == 1:
                    normalise1(1, 1)
                elif c == 2:
                    transposed1(1, 1)
            normalise1(2, 0)
            transposed1(2, 0)
            normalise1(3, 1)
            run_steps(act, 2, 2, NT - 2, NT, step1)

            def split_att(t):
                act.wait_ge(att_loaded, 16 * t + 16)
                wait(act, o_ps, 2 * t)
                nc.scalar.copy(at_h[:], at_in[:]).then_inc(at_hi, 1)

            def stack_to_sbuf(n, j, s):
                act.wait_ge(stack_ps, 5 * n + s + 1)
                dst = k_t[j][0:ST, :] if STACKS[s] == REP else q_t[j][0:ST, STACKS[s], :]
                nc.scalar.copy(dst, bank[0][0:ST, :]).then_inc(stack_sb, 1)

            def shift_to_stack(n, j, h):
                if h == 0:
                    act.wait_ge(shift_ps, n + 1)
                nc.scalar.copy(q_t[j][ST:P, h, :], bank[0][HD * h:HD * h + HD, :]).then_inc(shift_sb, 1)

            def exps(n, j, h, parts):
                for part in parts:
                    i = 3 * h + part
                    if i == 0:
                        wait(act, pv_ps, n - 1)
                        if isinstance(n, int) and n == 1:
                            for k in range(2):
                                act.wait_ge(qkv_stored[k], 16 * (NT // 2))
                    lo, w = ((0, 512), (512, 384), (896, 512))[part]
                    act.wait_ge(score_ps, UNITS * n + i + 1)
                    nc.scalar.activation(prob[j][:, h, lo:lo + w], bank[4 + i % 2][:, 0:w], ACT.Exp,
                                         scale=INV_SQRT_HD).then_inc(prob_ready, 1)

            def step2(n, j):
                here, after = live(n, 0, NG), live(n + 1, 0, NG)

                def stack_of(s):
                    if after:
                        stack_to_sbuf(n + 1, 1 - j, s)

                def first_stack(s):
                    if live(n + 2, 0, NG):
                        stack_to_sbuf(n + 2, j, s)

                def shift_of(h):
                    if here:
                        shift_to_stack(n, j, h)

                def exps_of(h, *parts):
                    if here:
                        exps(n, j, h, parts)

                shift_of(0)
                shift_of(1)
                exps_of(0, 0)
                shift_of(2)
                exps_of(0, 1)
                shift_of(3)
                exps_of(0, 2)
                stack_of(2)
                exps_of(1, 0, 1)
                stack_of(3)
                exps_of(1, 2)
                exps_of(2, 0)
                stack_of(4)
                exps_of(2, 1, 2)
                first_stack(0)
                exps_of(3, 0, 1, 2)
                first_stack(1)

            run_steps(act, -2, 2, NG - 2, NG - 1, step2)
            split_att(0)
            step2(NG - 1, 1)

            def normalise_y(t):
                act.wait_ge(y_scale, 8 * t + 4)
                nc.scalar.activation(y[:], y[:], ACT.Identity, bias=ln_nm[0][:], scale=ln_rs[0][:]
                                     ).then_inc(y_norm, 1)

            def normalise_x1(t, j):
                act.wait_ge(y_scale, 8 * t + 8)
                nc.scalar.activation(y[:], x1[j][:], ACT.Identity, bias=ln_nm[0][:], scale=ln_rs[0][:]
                                     ).then_inc(y_norm, 1)

            def transposed2(t):
                act.wait_ge(xt2_ps, t + 1)
                for h in range(2):
                    last = nc.scalar.copy(xt2_h[:, 4 * h:4 * h + 4, :].rearrange("p c t -> p (c t)"), bank[2 + h][:])
                last.then_inc(xt2_hi, 1)

            def gate(t):
                act.wait_ge(gate_step, 12 * t + 2)
                nc.scalar.activation(gate_e[:], logit[:], ACT.Exp, bias=neg_top[:]).then_inc(gate_exp, 1)

            def low_to_sbuf(t):
                act.wait_ge(low_ps, t + 1)
                nc.scalar.copy(low_h[:], bank[7][:, 0:P]).then_inc(low_hi, 1)

            def normalise_z(t, j):
                act.wait_ge(z_scale, 4 * t + 4)
                nc.scalar.activation(z[j][:], z[j][:], ACT.Identity, bias=ln_nm[1][:], scale=ln_rs[1][:]
                                     ).then_inc(z_norm, 1)

            def step3(t, j):
                if live(t, 0, NT):
                    transposed2(t)
                if live(t - 1, 0, NT):
                    low_to_sbuf(t - 1)
                    normalise_z(t - 1, 1 - j)
                if live(t + 2, 0, NT):
                    split_att(t + 2)
                if live(t + 1, 0, NT):
                    normalise_y(t + 1)
                    normalise_x1(t + 1, 1 - j)
                if live(t, 0, NT):
                    gate(t)

            act.wait_ge(pv_ps, NG)
            act.wait_ge(wo_ready, NG)
            for c in range(KC):
                act.wait_ge(wf_loaded[c % WF_RING], 16 * (c // WF_RING + 1))
                nc.scalar.copy(wf_h[c][:], raw_f[c % WF_RING][:]).then_inc(wf_hi, 1)
            split_att(1)
            normalise_y(0)
            normalise_x1(0, 0)
            act.wait_ge(wf_ready, KC)
            run_steps(act, 0, 2, NT - 2, NT + 1, step3)

        @block.vector
        def _(dve):
            def statistics(src, j, count, before_it):
                for h in range(2):
                    nc.vector.bn_stats(ln_st[j][:, h, :], src[:, HALF * h:HALF * h + HALF]).then_inc(count, 1)
                wait_apart(dve, count, before_it + 2, FIRST_X)
                nc.vector.bn_aggr(ln_mv[j][:], ln_st[j][:]).then_inc(count, 1)

            def stats1(t, j):
                dve.wait_ge(x_loaded[j], 16 * (t // 2) + 16)
                wait(dve, xn_ready, t - 1)
                statistics(x_in[j], j, ln1_step, 3 * t)

            def lo1(t, j):
                dve.wait_ge(xt_hi, t + 1)
                for h in range(2):
                    part = slice(4 * h, 4 * h + 4)
                    last = nc.vector.tensor_tensor(
                        xt_l[j][:, part, :].rearrange("p c t -> p (c t)"), bank[h][:],
                        xt_h[j][:, part, :].rearrange("p c t -> p (c t)").bitcast(F32), ALU.subtract)
                last.then_inc(xt_ready, 1)

            def bias(t, j):
                wait(dve, qkv_stored[j], 16 * (t // 2))
                flat = qkv[j][:].rearrange("p g c -> p (g c)")
                for n in range(3):
                    dve.wait_ge(proj_ps, 3 * t + n + 1)
                    cols = slice(HALF * n, HALF * n + HALF)
                    nc.vector.tensor_tensor(flat[:, cols], bank[2 + 3 * j + n][:], bq_row[:, cols], ALU.add
                                            ).then_inc(qkv_step, 1)

            def rope(t, j):
                qk = qkv[j][:, :, 0:QKW].rearrange("p g (h c) -> p g h c", c=HD)
                half = HD // 2
                tt = t % TT

                def table(tab, lo, hi):
                    row = tab[:, bass.ds(tt, 1), lo:hi]
                    return row.unsqueeze(1).broadcast_to([P, KV, REP + 1, hi - lo])

                dve.wait_ge(qkv_step, 7 * t + 3)
                nc.vector.tensor_tensor(rope_c[:], qk, table(cos_sb, 0, HD), ALU.mult).then_inc(qkv_step, 1)
                nc.vector.tensor_tensor(rope_s[:, :, :, 0:half], qk[:, :, :, half:HD], table(sin_sb, 0, half),
                                        ALU.mult).then_inc(qkv_step, 1)
                nc.vector.tensor_tensor(rope_s[:, :, :, half:HD], qk[:, :, :, 0:half], table(sin_sb, half, HD),
                                        ALU.mult).then_inc(qkv_step, 1)
                dve.wait_ge(qkv_step, 7 * t + 6)
                nc.vector.tensor_tensor(qk, rope_c[:], rope_s[:], ALU.add).then_inc(qkv_step, 1)

            def step1(t, j):
                lo1(t + 1, 1 - j)
                if live(t + 2, 0, NT):
                    stats1(t + 2, j)
                bias(t, j)
                rope(t, j)

            stats1(0, 0)
            for c in range(KC):
                dve.wait_ge(wq_hi, c + 1)
                nc.vector.tensor_tensor(wq_l[:, c, :], wq_raw[c % WQ_RING][:], wq_h[:, c, :].bitcast(F32),
                                        ALU.subtract).then_inc(wq_ready, 1)
                if c == 0:
                    stats1(1, 1)
                    lo1(0, 0)
                elif c == 2:
                    lo1(1, 1)
                elif c == 6:
                    stats1(2, 0)
            lo1(2, 0)
            dve.wait_ge(row_loaded, 16 * N_ROWS)
            bias(0, 0)
            rope(0, 0)
            stats1(3, 1)
            bias(1, 1)
            rope(1, 1)
            dve.wait_ge(ident_loaded, 16)
            nc.vector.tensor_copy(ident_r[:], ident[:]).then_inc(const_ready, 1)
            nc.vector.tensor_copy(ident_b[:], ident[:]).then_inc(const_ready, 1)
            nc.vector.tensor_copy(causal_b[:], causal[:]).then_inc(const_ready, 1)
            nc.vector.memset(ones[:], 1.0).then_inc(const_ready, 1)
            for j in range(2):
                nc.vector.memset(k_t[j][ST:P, :].bitcast(F32), 1.0).then_inc(const_ready, 1)
            run_steps(dve, 2, 2, NT - 2, NT - 2, step1)

            def split(n, j):
                dve.wait_ge(grp_loaded[j], 16 * (n // 2) + 16)
                wait(dve, stack_ps, 5 * (n - 1))
                qk = grp[j][:, :, 0:QKW].rearrange("p t (h c) -> p t h c", c=HD)
                q, k = qk[:, :, 0:REP, :], qk[:, :, REP, :]

                def slot(i):
                    return stack[j][:, :, :, HD * i:HD * i + HD]

                nc.vector.tensor_copy(slot(0), qk).then_inc(split_hi, 1)
                nc.vector.tensor_copy(slot(2)[:, :, 0:REP, :], q).then_inc(split_hi, 1)
                nc.vector.tensor_copy(slot(1)[:, :, REP, :], k).then_inc(split_hi, 1)

            def maxima(n, i):
                h, part = i // 3, i % 3
                if i == 0:
                    wait(dve, shift_step, 2 * n)
                dve.wait_ge(row_ps, UNITS * n + i + 1)
                for qb, at in (((0, 0), (1, 2 * P)), ((2, 0),), ((3, 0),))[part]:
                    last = nc.vector.tensor_reduce(neg_max[:, qb, h:h + 1], bank[1 + part][:, at:at + P * (qb + 1)],
                                                   AX_X, ALU.max, negate=True)
                last.then_inc(row_max, 1)

            def split_maxima(n):
                wait(dve, shift_ps, n)
                dve.wait_ge(row_max, UNITS * n + UNITS)
                nc.vector.tensor_copy(shift[:, :, :, 0], neg_max[:]).then_inc(shift_step, 1)
                dve.wait_ge(shift_step, 2 * n + 1)
                nc.vector.tensor_tensor(shift[:, :, :, 1], neg_max[:], shift[:, :, :, 0].bitcast(F32),
                                        ALU.subtract).then_inc(shift_step, 1)

            def turn_denominators(n):
                dve.wait_ge(den_ps, n + 1)
                nc.vector.transpose(den_t[:], bank[7][:]).then_inc(den_step, 1)

            def invert_denominators(n):
                dve.wait_ge(den_step, 3 * n + 1)
                nc.vector.reciprocal(den_r[:], den_t[:, 0:SEQ:HD]).then_inc(den_step, 1)

            def spread_inverses(n):
                dve.wait_ge(den_step, 3 * n + 2)
                nc.vector.transpose(den_i[:].rearrange("p (b c) -> p b c", c=HD),
                                    den_r[:].unsqueeze(2).broadcast_to([P, SEQ // HD, HD])).then_inc(den_step, 1)

            def quotient(n, j):
                dve.wait_ge(den_step, 3 * n + 3)
                dve.wait_ge(pv_ps, n + 1)
                wait(dve, att_stored[j], 16 * (n // 2))
                nc.vector.tensor_tensor(att[j][:], bank[6][:], den_i[:], ALU.mult).then_inc(att_ready, 1)

            def step2(n, j):
                after, before_it = live(n + 1, 0, NG), live(n - 1, 0, NG)

                def maxima_of(*units):
                    if after:
                        for i in units:
                            maxima(n + 1, i)

                if live(n - 2, 0, NG):
                    quotient(n - 2, j)
                if live(n + 2, 2, NG):
                    split(n + 2, j)
                maxima_of(0, 1, 2, 3, 4, 5)
                if before_it:
                    turn_denominators(n - 1)
                maxima_of(6)
                if before_it:
                    invert_denominators(n - 1)
                maxima_of(7)
                if before_it:
                    spread_inverses(n - 1)
                maxima_of(8, 9, 10, 11)
                if after:
                    split_maxima(n + 1)

            split(0, 0)
            step1(NT - 2, 0)
            split(1, 1)
            bias(NT - 1, 1)
            nc.vector.memset(shift[:].bitcast(F32), 0.0).then_inc(const_ready, 1)
            dve.wait_ge(const_ready, 7)
            step2(-1, 1)
            rope(NT - 1, 1)
            run_steps(dve, 0, 4, NG - 2, NG, step2)

            def split_att(t):
                dve.wait_ge(at_hi, t + 1)
                nc.vector.tensor_tensor(at_l[:], at_in[:], at_h[:].bitcast(F32), ALU.subtract).then_inc(at_ready, 1)

            split_att(0)
            step2(NG, 0)
            step2(NG + 1, 1)

            def project_sum(t):
                s = 9 * t
                wait(dve, xt2_ps, t)
                for n in range(2):
                    dve.wait_ge(o_ps, 2 * t + n + 1)
                    cols = slice(HALF * n, HALF * n + HALF)
                    nc.vector.tensor_tensor(y[:, cols], bank[n][:], bo_row[:, cols], ALU.add).then_inc(y_step, 1)
                dve.wait_ge(y_step, s + 2)
                statistics(y, 0, y_step, s + 2)

            def residual1(t, j):
                s = 9 * t
                dve.wait_ge(res_loaded, 16 * t + 16)
                dve.wait_ge(y_norm, 2 * t + 1)
                wait(dve, z_step, 7 * (t - 1))
                nc.vector.tensor_tensor(x1[j][:], y[:], x_res[:], ALU.add).then_inc(y_step, 1)
                dve.wait_ge(y_step, s + 6)
                statistics(x1[j], 0, y_step, s + 6)

            def lo2(t):
                dve.wait_ge(xt2_hi, t + 1)
                for h in range(2):
                    part = slice(4 * h, 4 * h + 4)
                    last = nc.vector.tensor_tensor(
                        xt2_l[:, part, :].rearrange("p c t -> p (c t)"), bank[2 + h][:],
                        xt2_h[:, part, :].rearrange("p c t -> p (c t)").bitcast(F32), ALU.subtract)
                last.then_inc(xt2_ready, 1)

            def gate(t):
                s = 12 * t

                def step(ins):
                    ins.then_inc(gate_step, 1)

                dve.wait_ge(ffn_ps, 3 * t + 1)
                step(nc.vector.tensor_copy(logit[:], bank[4][:, 0:EXP]))
                dve.wait_ge(gate_step, s + 1)
                mine = logit[:].unsqueeze(2).broadcast_to([P, EXP, EXP])
                other = logit[:].unsqueeze(1).broadcast_to([P, EXP, EXP])
                step(nc.vector.tensor_reduce(neg_top[:], logit[:], AX_X, ALU.max, negate=True))
                step(nc.vector.tensor_tensor(equal[:], other, mine, ALU.is_equal))
                step(nc.vector.tensor_tensor(later[:], other, mine, ALU.is_gt))
                dve.wait_ge(gate_step, s + 4)
                step(nc.vector.tensor_tensor(equal[:], equal[:], before[:], ALU.mult))
                dve.wait_ge(gate_step, s + 5)
                step(nc.vector.tensor_tensor(later[:], later[:], equal[:], ALU.add))
                dve.wait_ge(gate_step, s + 6)
                step(nc.vector.tensor_reduce(rank[:], later[:], AX_X, ALU.add))
                dve.wait_ge(gate_step, s + 7)
                dve.wait_ge(gate_exp, t + 1)
                step(nc.vector.scalar_tensor_tensor(out=gate_w[:], in0=rank[:], scalar=1.5, in1=gate_e[:],
                                                    op0=ALU.is_lt, op1=ALU.mult))
                dve.wait_ge(gate_step, s + 8)
                step(nc.vector.tensor_reduce(gate_s[:], gate_w[:], AX_X, ALU.add))
                dve.wait_ge(gate_step, s + 9)
                step(nc.vector.reciprocal(gate_r[:], gate_s[:]))
                dve.wait_ge(gate_step, s + 10)
                step(nc.vector.tensor_scalar(gate_w[:], gate_w[:], gate_r[:], SCALING, ALU.mult, ALU.mult))
                dve.wait_ge(gate_step, s + 11)
                wait(dve, low_ps, t)
                step(nc.vector.tensor_tensor(low[:], bank[4][:, EXP:AGW].rearrange("p (e r) -> p e r", r=RANK),
                                             gate_w[:].unsqueeze(2).broadcast_to([P, EXP, RANK]), ALU.mult))

            def low_lo(t):
                dve.wait_ge(low_hi, t + 1)
                nc.vector.tensor_tensor(low_l[:], bank[7][:, 0:P], low_h[:].bitcast(F32), ALU.subtract
                                        ).then_inc(low_ready, 1)

            def ffn_sum(t, j):
                s = 7 * t
                dve.wait_ge(lora_ps, t + 1)
                wait(dve, out_stored[j], 16 * (t // 2))
                for b, (at, w) in enumerate(FFN_COLS):
                    lo = max(at, AGW)
                    cols = slice(lo - AGW, at + w - AGW)
                    nc.vector.tensor_tensor(z[j][:, cols], bank[4 + b][:, lo - at:w], bf_row[:, cols], ALU.add
                                            ).then_inc(z_step, 1)
                dve.wait_ge(z_step, s + 3)
                statistics(z[j], 1, z_step, s + 3)

            def residual2(t, j):
                dve.wait_ge(z_norm, t + 1)
                nc.vector.tensor_tensor(z[j][:], z[j][:], x1[j][:], ALU.add).then_inc(z_step, 1)

            def step3(t, j):
                if live(t, 0, NT):
                    lo2(t)
                if live(t - 1, 0, NT):
                    low_lo(t - 1)
                    ffn_sum(t - 1, 1 - j)
                if live(t + 1, 0, NT):
                    project_sum(t + 1)
                if live(t - 1, 0, NT):
                    residual2(t - 1, 1 - j)
                if live(t + 2, 0, NT):
                    split_att(t + 2)
                if live(t + 1, 0, NT):
                    residual1(t + 1, 1 - j)
                if live(t, 0, NT):
                    gate(t)

            for c in range(KC):
                dve.wait_ge(wf_hi, c + 1)
                nc.vector.tensor_tensor(wf_l[c][:], raw_f[c % WF_RING][:], wf_h[c][:].bitcast(F32), ALU.subtract
                                        ).then_inc(wf_ready, 1)
            dve.wait_ge(late_loaded, 16 * N_LATE)
            for j in range(2):
                dve.wait_ge(att_stored[j], 16 * (NG // 2))
            project_sum(0)
            split_att(1)
            residual1(0, 0)
            run_steps(dve, 0, 4, NT - 2, NT + 1, step3)

        @block.tensor
        def _(pe):
            mm = nc.tensor.matmul

            def product(dst, a_h, a_l, w_h, w_l, start, stop):
                mm(dst, a_h, w_h, start=start, stop=False, skip_group_check=True)
                mm(dst, a_l, w_h, start=False, stop=False, skip_group_check=True)
                return mm(dst, a_h, w_l, start=False, stop=stop, skip_group_check=True)

            def transpose1(t, j):
                pe.wait_ge(xn_ready, t + 1)
                wait(pe, xt_ready, t)
                for c in range(KC):
                    last = nc.tensor.transpose(bank[c // 4][:, P * (c % 4):P * (c % 4) + P],
                                               xn[j][:, P * c:P * c + P], ident[:])
                last.then_inc(xt_ps, 1)

            def project_chunk(t, j, n, c):
                cols = slice(HALF * n, HALF * n + HALF)
                return product(bank[2 + 3 * j + n][:], xt_h[j][:, c, :], xt_l[j][:, c, :],
                               wq_h[:, c, cols], wq_l[:, c, cols], c == 0, c == KC - 1)

            def project_part(t, j, c):
                if c == 0:
                    pe.wait_ge(xt_ready, t + 1)
                pe.wait_ge(wq_ready, c + 1)
                for n in range(3):
                    last = project_chunk(t, j, n, c)
                    if c == KC - 1:
                        last.then_inc(proj_ps, 1)

            def project(t, j):
                pe.wait_ge(xt_ready, t + 1)
                for n in range(3):
                    pe.wait_ge(qkv_step, 7 * (t - 2) + n + 1)
                    for c in range(KC):
                        last = project_chunk(t, j, n, c)
                    last.then_inc(proj_ps, 1)

            def step1(t, j):
                if live(t + 1, 0, NT):
                    transpose1(t + 1, 1 - j)
                project(t, j)

            pe.wait_ge(ident_loaded, 16)
            transpose1(0, 0)
            project_part(0, 0, 0)
            transpose1(1, 1)
            project_part(0, 0, 1)
            for c in range(2, KC):
                project_part(0, 0, c)
                project_part(1, 1, c - 2)
            transpose1(2, 0)
            for c in range(KC - 2, KC):
                project_part(1, 1, c)
            run_steps(pe, 2, 2, NT - 2, NT, step1)

            pe.wait_ge(const_ready, 6)

            def stack_transpose(n, j, s):
                if s == 0:
                    pe.wait_ge(split_hi, 3 * n + 3)
                    pe.wait_ge(split_lo, 2 * n + 2)
                wait(pe, stack_sb, 5 * n + s)
                if s == 2:
                    wait(pe, shift_sb, 4 * n)
                head = STACKS[s]
                for tt in range(TT):
                    last = nc.tensor.transpose(bank[0][0:ST, P * tt:P * tt + P].bitcast(F32R),
                                               stack[j][:, tt, head, :], ident_r[:])
                last.then_inc(stack_ps, 1)

            def shift_transpose(n):
                pe.wait_ge(shift_step, 2 * n + 2)
                pe.wait_ge(stack_sb, min(5 * n + 7, 5 * NG) if isinstance(n, int) else 5 * n + 7)
                for tt in range(TT):
                    last = nc.tensor.transpose(bank[0][:, P * tt:P * tt + P].bitcast(F32R),
                                               shift[:, tt, :, :].rearrange("p h c -> p (h c)"), ident_r[:])
                last.then_inc(shift_ps, 1)

            def row_scores(n, j, i):
                h, part = i // 3, i % 3
                if part == 0:
                    pe.wait_ge(stack_sb, 5 * n + 2 + h)
                wait(pe, row_max, UNITS * n + i - 2)
                for qb, at in (((0, 0), (1, 2 * P)), ((2, 0),), ((3, 0),))[part]:
                    w = max(P * (qb + 1), 2 * P)
                    mm(bank[1 + part][:, at:at + w], q_t[j][0:ST, h, P * qb:P * qb + P], k_t[j][0:ST, 0:w],
                       start=True, stop=False, skip_group_check=True)
                    diag = slice(at + P * qb, at + P * qb + P)
                    last = mm(bank[1 + part][:, diag], ident_b[:], causal_b[:], start=False, stop=True,
                              skip_group_check=True)
                last.then_inc(row_ps, 1)

            def scores(n, j, i):
                h, part = i // 3, i % 3
                if part == 0:
                    pe.wait_ge(shift_sb, 4 * n + h + 1)
                wait(pe, prob_ready, UNITS * n + i - 1)
                for kc, at, q0 in (((0, 0, 0),), ((1, 0, P),), ((2, 0, 2 * P), (3, 2 * P, 2 * P)))[part]:
                    w = SEQ - q0
                    last = mm(bank[4 + i % 2][:, at:at + w], k_t[j][:, P * kc:P * kc + P], q_t[j][:, h, q0:SEQ],
                              start=True, stop=True, skip_group_check=True)
                last.then_inc(score_ps, 1)

            def weigh(n, j, kc, values):
                if kc == 0:
                    if values:
                        wait(pe, att_ready, n)
                        pe.wait_ge(v_loaded[j], 16 * (n // 2) + 16)
                    else:
                        pe.wait_ge(prob_masked, 8 * n + 8)
                        wait(pe, den_step, 3 * n - 2)
                at = (0, 512, 896, 1280)[kc]
                w = SEQ - P * kc
                dst = bank[6] if values else bank[7]
                for h in range(REP):
                    last = mm(dst[HD * h:HD * h + HD, P * kc:SEQ], v_sb[j][:, kc, :] if values else ones[:],
                              prob[j][:, h, at:at + w], start=(kc == 0), stop=(kc == TT - 1), skip_group_check=True)
                if kc == TT - 1:
                    last.then_inc(pv_ps if values else den_ps, 1)

            order = ("T0 D0 C0 R0 C1 D1 R1 C2 R2 S2 C3 D2 R3 C4 S3 R4 C5 D3 R5 C6 V0 R6 S4 C7 R7 C8 N0 R8 C9 "
                     "V1 R9 C10 R10 C11 N1 R11 V2 V3").split()

            def step2(n, j):
                before_it, here, after = live(n - 1, 0, NG), live(n, 0, NG), live(n + 1, 0, NG)
                for what in order:
                    kind, i = what[0], int(what[1:])
                    if kind == "S" and after:
                        stack_transpose(n + 1, 1 - j, i)
                    if kind == "N" and live(n + 2, 0, NG):
                        stack_transpose(n + 2, j, i)
                    if kind == "R" and after:
                        row_scores(n + 1, 1 - j, i)
                    if kind == "T" and here:
                        shift_transpose(n)
                    if kind == "C" and here:
                        scores(n, j, i)
                    if kind in "DV" and before_it:
                        weigh(n - 1, 1 - j, i, kind == "V")

            pe.wait_ge(qkv_step, 7 * (NT - 2) + 3)
            run_steps(pe, -2, 2, NG - 2, NG + 1, step2)

            def project_out(t, n):
                if n == 0:
                    pe.wait_ge(at_ready, t + 1)
                wait(pe, y_step, 9 * (t - 1) + n + 1)
                for c in range(KC):
                    cols = slice(D * c + HALF * n, D * c + HALF * n + HALF)
                    last = product(bank[n][:], at_h[:, c, :], at_l[:, c, :], wo_h[:, cols], wo_l[:, cols],
                                   c == 0, c == KC - 1)
                last.then_inc(o_ps, 1)

            def transpose2(t):
                pe.wait_ge(y_norm, 2 * t + 2)
                wait(pe, xt2_ready, t)
                for c in range(KC):
                    last = nc.tensor.transpose(bank[2 + c // 4][:, P * (c % 4):P * (c % 4) + P],
                                               y[:, P * c:P * c + P], ident[:])
                last.then_inc(xt2_ps, 1)

            def ffn(t):
                pe.wait_ge(xt2_ready, t + 1)
                wait(pe, z_step, 7 * (t - 1) + 3)
                for b, (at, w) in enumerate(FFN_COLS):
                    for c in range(KC):
                        if isinstance(t, int) and t == 0 and b == 0:
                            pe.wait_ge(wf_ready, c + 1)
                        last = product(bank[4 + b][:, 0:w], xt2_h[:, c, :], xt2_l[:, c, :], wf_h[c][:, at:at + w],
                                       wf_l[c][:, at:at + w], c == 0, False)
                    last.then_inc(ffn_ps, 1)

            def transpose_low(t):
                pe.wait_ge(gate_step, 12 * t + 12)
                wait(pe, low_ready, t)
                nc.tensor.transpose(bank[7][:, 0:P], low[:].rearrange("p e r -> p (e r)"), ident[:]).then_inc(low_ps, 1)

            def lora(t):
                pe.wait_ge(low_ready, t + 1)
                for b, (at, w) in enumerate(FFN_COLS):
                    lo = max(at, AGW)
                    cols = slice(KC * D + lo - AGW, KC * D + at + w - AGW)
                    last = product(bank[4 + b][:, lo - at:w], low_h[:], low_l[:], wo_h[:, cols], wo_l[:, cols],
                                   False, True)
                last.then_inc(lora_ps, 1)

            def step3(t, j):
                transpose2(t)
                if live(t - 1, 0, NT):
                    transpose_low(t - 1)
                if live(t + 1, 2, NT):
                    project_out(t + 1, 0)
                if live(t - 1, 0, NT):
                    lora(t - 1)
                if live(t + 1, 2, NT):
                    project_out(t + 1, 1)
                ffn(t)

            pe.wait_ge(wo_ready, NG)
            for t in range(2):
                for n in range(2):
                    project_out(t, n)
            run_steps(pe, 0, 2, NT - 2, NT, step3)
            transpose_low(NT - 1)
            lora(NT - 1)


def kernel(L0_attn_x, L0_attn_w_qkv, L0_attn_b_qkv, L0_attn_w_o, L0_attn_b_o, L0_ffn_gate_w, L0_ffn_base_w,
           L0_ffn_base_b, L0_ffn_lora_A, L0_ffn_lora_B):
    import numpy as np
    import concourse.bacc as bacc
    from concourse import mybir as mb
    from concourse.bass_utils import run_bass_kernel_spmd

    halves = np.concatenate([np.arange(0, HD, 2), np.arange(1, HD, 2)])
    order = []
    for g in range(KV):
        for h in range(REP):
            order.append((REP * g + h) * HD + halves)
        order.append(HEADS * HD + g * HD + halves)
        order.append((HEADS + KV) * HD + g * HD + np.arange(HD))
    order = np.concatenate(order)

    def by_partition(w_t):
        return np.ascontiguousarray(w_t.reshape(KC, P, -1).transpose(1, 0, 2))

    arr = {k: np.asarray(v) for k, v in locals().items() if k.startswith("L0_")}
    w_qkv = by_partition(arr["L0_attn_w_qkv"][order].T)
    w_o = by_partition(arr["L0_attn_w_o"].T).reshape(P, KC * D)
    lora_b = arr["L0_ffn_lora_B"].transpose(0, 2, 1).reshape(ER, D)
    w_ffn = np.concatenate([arr["L0_ffn_gate_w"].T, arr["L0_ffn_lora_A"].reshape(ER, D).T, arr["L0_ffn_base_w"].T], 1)

    inv = np.float32(1.0) / np.float32(10000.0) ** (np.arange(0, HD, 2, dtype=np.float32) / np.float32(HD))
    ang = np.arange(SEQ, dtype=np.float32)[:, None] * inv[None, :].astype(np.float32)
    cos, sin = np.cos(ang).astype(np.float32), np.sin(ang).astype(np.float32)

    def table(t):
        return np.ascontiguousarray(t.reshape(TT, P, HD).transpose(1, 0, 2))

    inputs = {
        "x": np.ascontiguousarray(arr["L0_attn_x"].reshape(NT, P, D)),
        "w_qkv": w_qkv,
        "b_qkv": np.ascontiguousarray(arr["L0_attn_b_qkv"][order][None]),
        "w_out": np.ascontiguousarray(np.concatenate([w_o, lora_b], 1)),
        "b_o": np.ascontiguousarray(arr["L0_attn_b_o"][None]),
        "w_ffn": by_partition(w_ffn),
        "b_ffn": np.ascontiguousarray(arr["L0_ffn_base_b"][None]),
        "cos_t": table(np.concatenate([cos, cos], 1)),
        "sin_t": table(np.concatenate([-sin, sin], 1)),
        "ident": np.eye(P, dtype=np.float32),
        "causal": np.where(np.tril(np.ones((P, P), bool)), 0.0, MASKED).astype(np.float32),
        "before": np.tril(np.ones((EXP, EXP), np.float32), -1)[None],
    }
    nc = bacc.Bacc("TRN2", target_bir_lowering=False, num_devices=1)
    aps = [nc.dram_tensor(k, v.shape, mb.dt.from_np(v.dtype), kind="ExternalInput").ap() for k, v in inputs.items()]
    out = nc.dram_tensor("out", (NT, P, D), mb.dt.float32, kind="ExternalOutput").ap()
    build(nc, *aps, out)
    result = run_bass_kernel_spmd(nc, [inputs], core_ids=[0])
    return result.results[0]["out"].reshape(BATCH, SEQ, D)
```

```python
from contextlib import ExitStack

import concourse.bass as bass
from concourse import mybir

F32 = mybir.dt.float32
F32R = mybir.dt.float32r
BF16 = mybir.dt.bfloat16
ALU = mybir.AluOpType
ACT = mybir.ActivationFunctionType
AX_X = mybir.AxisListType.X

P = 128
D = 1024
KC = D // P
BATCH, SEQ = 4, 512
NT = BATCH * SEQ // P
TT = SEQ // P
HEADS, KV, HD = 32, 8, 32
REP = HEADS // KV
GW = (REP + 2) * HD
QKW = (REP + 1) * HD
QKV = KV * GW
NG = BATCH * KV
EXP, RANK = 8, 16
ER = EXP * RANK
AGW = EXP + ER
FW = AGW + D
EPS = 1e-5
SCALING = 2.0
INV_SQRT_HD = float(HD) ** -0.5
HALF = 512
MASKED = -1.0e30
STACKS = (0, REP, 1, 2, 3)
ST = 3 * HD
OUT_SPLIT = (KC + 1) * D
PIECE = OUT_SPLIT // NG
FFN_COLS = [(0, AGW + 256), (AGW + 256, 384), (AGW + 640, 384)]
WQ_RING = 4
WF_RING = 4
EARLY = 3
UNITS = 3 * REP


def wait(eng, sem, value):
    if not (isinstance(value, int) and value <= 0):
        eng.wait_ge(sem, value)


def wait_apart(eng, sem, value, passed):
    if not (isinstance(value, int) and value <= 0):
        if not isinstance(value, int):
            eng.compute_val(value)
            eng.wait_ge(*passed)
        eng.wait_ge(sem, value)


def live(n, lo, hi):
    return not isinstance(n, int) or lo <= n < hi


def only(n, value):
    return isinstance(n, int) and n == value


def final_cols(t):
    return [slice(0, HALF), slice(HALF, D)] if only(t, NT - 1) else [slice(0, D)]


def run_steps(eng, first, lo, hi, last, step):
    for n in range(first, lo):
        step(n, n % 2)
    with eng.Fori(lo // 2, hi // 2) as i:
        for j in range(2):
            step(2 * i + j, j)
    for n in range(hi, last):
        step(n, n % 2)


def build(nc, x, w_qkv, b_qkv, w_out, b_o, w_ffn, b_ffn, cos_t, sin_t, ident_h, causal_h, before_h, out):
    qkv_scratch = nc.dram_tensor("qkv_scratch", [NT, P, QKV], F32).ap()
    att_scratch = nc.dram_tensor("att_scratch", [NG // KV, KV, P, SEQ], F32).ap()

    with ExitStack() as ctx:
        arena_bytes, arena_at = 212000, 16512
        ctx.enter_context(nc.sbuf_tensor("arena", [P, arena_bytes], mybir.dt.uint8))
        start = arena_at + 128
        limit = arena_at + arena_bytes

        def sem(name):
            return ctx.enter_context(nc.semaphore(name))

        class Map:

            def __init__(self, at):
                self.at = at

            def __call__(self, name, shape, dtype=F32):
                size = mybir.dt.size(dtype)
                for n in shape[1:]:
                    size *= n
                t = nc.alloc_sbuf_tensor_at(name, shape, dtype, offset=self.at)
                self.at += -(-size // 32) * 32
                assert self.at <= limit, (name, self.at - limit)
                return t

        m = Map(start)
        ident = m("ident", [P, P])
        ident_r = m("ident_r", [P, P], F32R)
        ident_b = m("ident_b", [P, P], BF16)
        causal_b = m("causal_b", [P, P], BF16)
        causal = m("causal", [P, P])
        ones = m("ones", [P, HD])
        before = m("before", [P, EXP, EXP])
        bo_row = m("bo_row", [P, D])
        bf_row = m("bf_row", [P, D])
        ln_st = [m(f"ln_st{j}", [P, 2, 6]) for j in range(2)]
        ln_mv = [m(f"ln_mv{j}", [P, 2]) for j in range(2)]
        ln_rs = [m(f"ln_rs{j}", [P, 1]) for j in range(2)]
        ln_nm = [m(f"ln_nm{j}", [P, 1]) for j in range(2)]
        ln_ve = [m(f"ln_ve{j}", [P, 1]) for j in range(2)]
        ln_mm = [m(f"ln_mm{j}", [P, 1]) for j in range(2)]
        minus_half = m("minus_half", [P, 1])
        minus_one = m("minus_one", [P, 1])
        eps_col = m("eps_col", [P, 1])
        den_r = m("den_r", [P, SEQ // HD])
        common_end = m.at

        phase1_at = common_end
        m = Map(phase1_at)
        wq_h = m("wq_h", [P, KC, QKV], F32R)
        wq_l = m("wq_l", [P, KC, QKV], F32R)
        wq_raw = [m(f"wq_raw{j}", [P, QKV]) for j in range(WQ_RING)]
        wq_end = m.at

        m = Map(phase1_at)
        wo_h = m("wo_h", [P, OUT_SPLIT], F32R)
        wo_l = m("wo_l", [P, OUT_SPLIT], F32R)
        phase3_at = m.at
        prob = [m("prob0", [P, REP, 1408])]
        z_at = m.at
        den_t = m("den_t", [P, SEQ])
        den_i = m("den_i", [P, SEQ])
        att = [m(f"att{j}", [P, SEQ]) for j in range(2)]
        raw_at = m.at
        grp = [m(f"grp{j}", [P, TT, GW]) for j in range(2)]
        stack = [m(f"stack{j}", [P, TT, REP + 1, ST], F32R) for j in range(2)]
        raw_limit = m.at
        v_sb = [m(f"v_sb{j}", [P, TT, HD]) for j in range(2)]
        wo_raw = [m(f"wo_raw{j}", [P, PIECE]) for j in range(2)]
        k_t = [m(f"k_t{j}", [P, SEQ], F32R) for j in range(2)]
        m.at = max(m.at, wq_end)
        x_at = m.at
        q_t = [m(f"q_t{j}", [P, REP, SEQ], F32R) for j in range(2)]
        shift = m("shift", [P, TT, REP, HD], F32R)
        neg_max = m("neg_max", [P, TT, REP])
        prob1_at = m.at
        prob.append(m("prob1", [P, REP, 1408]))
        phase2_end = m.at

        m = Map(x_at)
        x_in = [m(f"x_in{j}", [P, D]) for j in range(2)]
        xn = [m(f"xn{j}", [P, D]) for j in range(2)]
        xt_h = [m(f"xt_h{j}", [P, KC, P], F32R) for j in range(2)]
        xt_l = [m(f"xt_l{j}", [P, KC, P], F32R) for j in range(2)]
        qkv = [m(f"qkv{j}", [P, KV, GW]) for j in range(2)]
        qkv_end = m.at

        m = Map(phase3_at)
        x1 = [m(f"x1_{j}", [P, D]) for j in range(2)]
        y = m("y", [P, D])
        wf_h, wf_l = [None] * KC, [None] * KC
        wf_h[0] = m("wf_h0", [P, FW], F32R)
        at1_l = m("at1_l", [P, KC, P], F32R)
        low = m("low", [P, EXP, RANK])
        later = m("later", [P, EXP, EXP])
        equal = m("equal", [P, EXP, EXP])
        assert m.at <= z_at
        m = Map(phase3_at + D * 4)
        at1_h = m("at1_h", [P, KC, P], F32R)
        m = Map(z_at)
        z = [m(f"z{j}", [P, D]) for j in range(2)]
        assert m.at <= raw_at
        m = Map(raw_at)
        raw_f = [m(f"raw_f{j}", [P, FW]) for j in range(WF_RING)]
        assert m.at <= raw_limit
        m = Map(raw_at)
        xt2_h = m("xt2_h", [P, KC, P], F32R)
        xt2_l = m("xt2_l", [P, KC, P], F32R)
        low_h = m("low_h", [P, P], F32R)
        low_l = m("low_l", [P, P], F32R)
        m = Map(raw_at + 2 * FW * 4)
        wf_l[KC - 2] = m(f"wf_l{KC - 2}", [P, FW], F32R)
        wf_l[KC - 1] = m(f"wf_l{KC - 1}", [P, FW], F32R)
        wf_l[KC - 3] = m(f"wf_l{KC - 3}", [P, FW], F32R)
        wf_l[0] = m("wf_l0", [P, FW], F32R)
        for c in range(1, KC):
            if c == EARLY:
                assert m.at <= prob1_at
            wf_h[c] = m(f"wf_h{c}", [P, FW], F32R)
            if c < KC - 4:
                wf_l[c] = m(f"wf_l{c}", [P, FW], F32R)
        m = Map(max(m.at, phase2_end, qkv_end))
        tables_at = m.at
        at_in = m("at_in", [P, KC, P])
        at_h = m("at_h", [P, KC, P], F32R)
        at_l_at = m.at
        at_l = m("at_l", [P, KC, P], F32R)
        x_res = m("x_res", [P, D])
        last_at = m.at
        wf_l[KC - 4] = m(f"wf_l{KC - 4}", [P, FW], F32R)
        logit = m("logit", [P, EXP])
        rank = m("rank", [P, EXP])
        neg_top = m("neg_top", [P, 1])
        gate_e = m("gate_e", [P, EXP])
        gate_w = m("gate_w", [P, EXP])
        gate_s = m("gate_s", [P, 1])
        gate_r = m("gate_r", [P, 1])

        key_sum = [Map(at)(f"key_sum{j}", [P, REP, 2 * P]) for j, at in enumerate((at_l_at, last_at))]

        m = Map(tables_at)
        rope_c = m("rope_c", [P, KV, REP + 1, HD])
        cos_sb = m("cos_sb", [P, TT, HD])
        sin_sb = m("sin_sb", [P, TT, HD])
        bq_row = m("bq_row", [P, QKV])
        rope_s = m("rope_s", [P, KV, REP + 1, HD])

        bank = [ctx.enter_context(nc.psum_tensor(f"bank{i}", [P, HALF], F32)) for i in range(8)]

        ident_loaded = sem("ident_loaded")
        row_loaded = sem("row_loaded")
        late_loaded = sem("late_loaded")
        const_ready = sem("const_ready")
        wq_loaded = [sem(f"wq_loaded{j}") for j in range(WQ_RING)]
        wq_hi = sem("wq_hi")
        wq_ready = sem("wq_ready")
        x_loaded = [sem(f"x_loaded{j}") for j in range(2)]
        ln1_step = sem("ln1_step")
        ln1_norm = sem("ln1_norm")
        half_set = sem("half_set")
        xn_ready = sem("xn_ready")
        xt_ps = sem("xt_ps")
        xt_hi = sem("xt_hi")
        xt_ready = sem("xt_ready")
        proj_ps = sem("proj_ps")
        qkv_step = sem("qkv_step")
        qkv_stored = [sem(f"qkv_stored{j}") for j in range(2)]
        grp_loaded = [sem(f"grp_loaded{j}") for j in range(2)]
        v_loaded = [sem(f"v_loaded{j}") for j in range(2)]
        wo_loaded = [sem(f"wo_loaded{j}") for j in range(2)]
        wo_hi = sem("wo_hi")
        wo_ready = sem("wo_ready")
        split_hi = sem("split_hi")
        split_lo = sem("split_lo")
        stack_ps = sem("stack_ps")
        stack_sb = sem("stack_sb")
        row_ps = sem("row_ps")
        row_max_0 = sem("row_max_0")
        row_max = sem("row_max")
        shift_step = sem("shift_step")
        shift_ps = sem("shift_ps")
        shift_sb = sem("shift_sb")
        score_ps = sem("score_ps")
        prob_ready = sem("prob_ready")
        prob_masked = sem("prob_masked")
        prob_summed = sem("prob_summed")
        den_ps = sem("den_ps")
        den_step = sem("den_step")
        pv_ps = sem("pv_ps")
        att_ready = sem("att_ready")
        att_stored = [sem(f"att_stored{j}") for j in range(2)]
        wf_loaded = [sem(f"wf_loaded{j}") for j in range(WF_RING)]
        wf_hi = sem("wf_hi")
        wf_ready = sem("wf_ready")
        att_loaded = sem("att_loaded")
        res_loaded = sem("res_loaded")
        at_hi = sem("at_hi")
        at_ready = sem("at_ready")
        o_ps = sem("o_ps")
        y_step = sem("y_step")
        y_scale = sem("y_scale")
        y_norm = sem("y_norm")
        xt2_ps = sem("xt2_ps")
        xt2_hi = sem("xt2_hi")
        xt2_ready = sem("xt2_ready")
        ffn_ps = sem("ffn_ps")
        gate_step = sem("gate_step")
        gate_exp = sem("gate_exp")
        low_ps = sem("low_ps")
        low_hi = sem("low_hi")
        low_ready = sem("low_ready")
        lora_ps = sem("lora_ps")
        z_step = sem("z_step")
        z_scale = sem("z_scale")
        z_norm = sem("z_norm")
        out_stored = [sem(f"out_stored{j}") for j in range(2)]

        block = ctx.enter_context(nc.Block())

        N_ROWS = 4
        N_LATE = 3
        FIRST_X = (x_loaded[0], 16)

        @block.sync
        def _(sp):
            sp.dma_start(x_in[0][:], x[0]).then_inc(x_loaded[0], 16)
            sp.dma_start(ident[:], ident_h).then_inc(ident_loaded, 16)
            sp.dma_start(wq_raw[0][:], w_qkv[:, 0, :]).then_inc(wq_loaded[0], 16)
            sp.dma_start(x_in[1][:], x[1]).then_inc(x_loaded[1], 16)
            for c in range(1, WQ_RING):
                sp.dma_start(wq_raw[c][:], w_qkv[:, c, :]).then_inc(wq_loaded[c], 16)

            def load_x(t, j):
                wait_apart(sp, xn_ready, t - 1, FIRST_X)
                sp.dma_start(x_in[j][:], x[t]).then_inc(x_loaded[j], 16)

            for c in range(WQ_RING, KC):
                if c == KC - 1:
                    load_x(2, 0)
                sp.wait_ge(wq_ready, c - WQ_RING + 1)
                sp.dma_start(wq_raw[c % WQ_RING][:], w_qkv[:, c, :]).then_inc(wq_loaded[c % WQ_RING], 16)
            sp.dma_start(bq_row[:], b_qkv[0].partition_broadcast(P)).then_inc(row_loaded, 16)
            sp.dma_start(cos_sb[:], cos_t).then_inc(row_loaded, 16)
            sp.dma_start(sin_sb[:], sin_t).then_inc(row_loaded, 16)
            sp.dma_start(causal[:], causal_h).then_inc(row_loaded, 16)
            load_x(3, 1)
            load_x(4, 0)
            sp.dma_start(before[:], before_h[0].partition_broadcast(P)).then_inc(late_loaded, 16)
            sp.dma_start(bo_row[:], b_o[0].partition_broadcast(P)).then_inc(late_loaded, 16)
            sp.dma_start(bf_row[:], b_ffn[0].partition_broadcast(P)).then_inc(late_loaded, 16)

            def store_qkv(t, j):
                wait_apart(sp, qkv_step, 7 * t + 7, FIRST_X)
                sp.dma_start(qkv_scratch[t], qkv[j][:].rearrange("p g c -> p (g c)")).then_inc(qkv_stored[j], 16)

            def io1(t, j):
                if live(t + 3, 5, NT):
                    load_x(t + 3, 1 - j)
                store_qkv(t, j)

            def group(n):
                return n // KV, n % KV

            def load_group(n, j):
                b, g = group(n)
                wait_apart(sp, split_hi, 3 * (n - 1), FIRST_X)
                wait(sp, split_lo, 2 * (n - 1))
                if isinstance(n, int):
                    for i in range(2):
                        sp.wait_ge(qkv_stored[i], 16 * TT // 2 * (b + 1))
                src = qkv_scratch.rearrange("(b t) p (g c) -> b g p t c", t=TT, c=GW)[b, g]
                sp.dma_start(grp[j][:], src).then_inc(grp_loaded[j], 16)

            def load_v(n, j):
                b, g = group(n)
                wait_apart(sp, pv_ps, n - 1, FIRST_X)
                src = qkv_scratch.rearrange("(b t) p (g c) -> b g p t c", t=TT, c=GW)[b, g][:, :, QKW:GW]
                sp.dma_start(v_sb[j][:], src).then_inc(v_loaded[j], 16)

            def load_piece(n, j):
                wait_apart(sp, wo_ready, n - 1, FIRST_X)
                src = w_out.rearrange("p (n c) -> n p c", c=PIECE)[n]
                sp.dma_start(wo_raw[j][:], src).then_inc(wo_loaded[j], 16)

            def store_att(n, j):
                b, g = group(n)
                wait_apart(sp, att_ready, n + 1, FIRST_X)
                sp.dma_start(att_scratch[b, g], att[j][:]).then_inc(att_stored[j], 16)

            def io2(n, j):
                if live(n + 3, 2, NG):
                    load_group(n + 3, 1 - j)
                if live(n - 2, 0, NG):
                    store_att(n - 2, j)
                if live(n + 2, 2, NG):
                    load_piece(n + 2, j)
                if live(n + 1, 2, NG):
                    load_v(n + 1, 1 - j)

            run_steps(sp, 0, 2, NT - 4, NT - 4, io1)
            load_piece(0, 0)
            load_piece(1, 1)
            load_group(0, 0)
            load_group(1, 1)
            load_v(0, 0)
            load_v(1, 1)
            for t in range(NT - 4, NT - 1):
                io1(t, t % 2)
            io2(-1, 1)
            io2(0, 0)
            store_qkv(NT - 1, 1)
            for i in range(2):
                sp.wait_ge(qkv_stored[i], 16 * (NT // 2))
            run_steps(sp, 1, 2, NG - 4, NG - 2, io2)

            def load_att(t):
                wait_apart(sp, at_ready, t, FIRST_X)
                for i in range(2):
                    wait(sp, att_stored[i], 16 * KV // 2 * (t // TT + 1))
                src = att_scratch.rearrange("b g p (t c) -> b t p g c", c=P)[t // TT, t % TT]
                sp.dma_start(at_in[:], src).then_inc(att_loaded, 16)

            def load_res(t):
                wait_apart(sp, y_step, 9 * (t - 1) + 6, FIRST_X)
                sp.dma_start(x_res[:], x[t]).then_inc(res_loaded, 16)

            def load_ffn(c):
                wait(sp, wf_ready, c - WF_RING + 1)
                sp.dma_start(raw_f[c % WF_RING][:], w_ffn[:, c, :]).then_inc(wf_loaded[c % WF_RING], 16)

            def store_out(t, j):
                for i, cols in enumerate(final_cols(t)):
                    wait_apart(sp, z_step, 7 * t + 7 + i, FIRST_X)
                    sp.dma_start(out[t][:, cols], z[j][:, cols]).then_inc(out_stored[j], 16)

            load_att(0)
            load_res(0)
            io2(NG - 2, 0)
            io2(NG - 1, 1)
            sp.wait_ge(stack_ps, 5 * NG)
            sp.wait_ge(split_lo, 2 * NG)
            for c in range(WF_RING):
                load_ffn(c)
            load_att(1)
            io2(NG, 0)
            for c in range(WF_RING, WF_RING + EARLY):
                load_ffn(c)
            io2(NG + 1, 1)
            for c in range(WF_RING + EARLY, KC):
                load_ffn(c)
            load_res(1)

            def io3(t, j):
                if live(t + 2, 0, NT):
                    load_att(t + 2)
                if live(t - 1, 0, NT):
                    store_out(t - 1, 1 - j)
                if live(t + 2, 0, NT):
                    load_res(t + 2)

            run_steps(sp, 0, 2, NT - 2, NT + 1, io3)
            sp.wait_ge(out_stored[0], 16 * (NT // 2))
            sp.wait_ge(out_stored[1], 16 * (NT // 2 + 1))

        @block.gpsimd
        def _(pool):
            def scale_and_shift(j, count, before_it):
                nc.gpsimd.tensor_tensor(ln_ve[j][:], ln_mv[j][:, 1:2], eps_col[:], ALU.add).then_inc(count, 1)
                nc.gpsimd.tensor_tensor(ln_mm[j][:], ln_mv[j][:, 0:1], minus_one[:], ALU.mult).then_inc(count, 1)
                pool.wait_ge(count, before_it + 1)
                nc.gpsimd.tensor_tensor(ln_rs[j][:], ln_ve[j][:], minus_half[:], ALU.pow).then_inc(count, 1)
                pool.wait_ge(count, before_it + 3)
                nc.gpsimd.tensor_tensor(ln_nm[j][:], ln_mm[j][:], ln_rs[j][:], ALU.mult).then_inc(count, 1)

            def scale1(t, j):
                pool.wait_ge(ln1_step, 3 * t + 3)
                scale_and_shift(j, ln1_norm, 4 * t)

            nc.gpsimd.memset(minus_half[:], -0.5).then_inc(half_set, 1)
            nc.gpsimd.memset(minus_one[:], -1.0).then_inc(half_set, 1)
            nc.gpsimd.memset(eps_col[:], EPS).then_inc(half_set, 1)
            pool.wait_ge(half_set, 3)
            run_steps(pool, 0, 2, NT, NT, scale1)

            def mask(n, j, h):
                wait_apart(pool, prob_ready, UNITS * n + 3 * h + 3, (half_set, 3))
                d0 = prob[j][:, h, 0:P]
                nc.gpsimd.affine_select(out=d0, in_=d0, compare_op=ALU.is_ge, fill=0.0, base=0,
                                        pattern=[[1, P]], channel_multiplier=-1).then_inc(prob_masked, 1)
                d1 = prob[j][:, h, 512:1408].rearrange("p (a c) -> p a c", c=P)[:, 0:7:3, :]
                nc.gpsimd.affine_select(out=d1, in_=d1, compare_op=ALU.is_ge, fill=0.0, base=0,
                                        pattern=[[0, 3], [1, P]], channel_multiplier=-1).then_inc(prob_masked, 1)

            def add_keys(n, j, h):
                total, p = key_sum[j][:, h, :], prob[j][:, h, :]
                pool.wait_ge(prob_masked, 8 * n + 2 * h + 2)
                wait(pool, den_ps, n - 1)
                if only(n, 1):
                    pool.wait_ge(qkv_step, 7 * NT)
                nc.gpsimd.tensor_tensor(total, p[:, 640:896], p[:, 896:1152], ALU.add).then_inc(prob_summed, 1)
                pool.wait_ge(prob_summed, 8 * n + 2 * h + 1)
                nc.gpsimd.tensor_tensor(total[:, P:], total[:, P:], p[:, 1280:1408], ALU.add).then_inc(prob_summed, 1)

            def piece_lo(n, j):
                hi = wo_h[:, bass.ds(n * PIECE, PIECE)]
                lo = wo_l[:, bass.ds(n * PIECE, PIECE)]
                pool.wait_ge(wo_hi, n + 1)
                nc.gpsimd.tensor_tensor(lo, wo_raw[j][:], hi.bitcast(F32), ALU.subtract).then_inc(wo_ready, 1)

            def split_group(n, j):
                pool.wait_ge(split_hi, 3 * n + 3)
                qk = grp[j][:, :, 0:QKW].rearrange("p t (h c) -> p t h c", c=HD)
                hi = stack[j][:, :, :, 0:HD].bitcast(F32)
                nc.gpsimd.tensor_tensor(stack[j][:, :, 0:REP, HD:2 * HD], qk[:, :, 0:REP, :], hi[:, :, 0:REP, :],
                                        ALU.subtract).then_inc(split_lo, 1)
                nc.gpsimd.tensor_tensor(stack[j][:, :, REP, 2 * HD:ST], qk[:, :, REP, :], hi[:, :, REP, :],
                                        ALU.subtract).then_inc(split_lo, 1)

            def step2(n, j):
                if live(n + 2, 0, NG):
                    split_group(n + 2, j)
                for h in range(REP):
                    mask(n, j, h)
                    add_keys(n, j, h)
                    if h == (1 if only(n, NG - 1) else REP - 1):
                        piece_lo(n, j)

            split_group(0, 0)
            split_group(1, 1)
            run_steps(pool, 0, 2, NG - 2, NG, step2)

            def scale_y(t):
                pool.wait_ge(y_step, 9 * t + 5)
                wait(pool, y_norm, 2 * t)
                scale_and_shift(0, y_scale, 8 * t)
                pool.wait_ge(y_step, 9 * t + 9)
                scale_and_shift(0, y_scale, 8 * t + 4)

            def scale_z(t):
                pool.wait_ge(z_step, 7 * t + 6)
                scale_and_shift(1, z_scale, 4 * t)

            def step3(t, j):
                if live(t - 1, 0, NT):
                    scale_z(t - 1)
                if live(t + 1, 0, NT):
                    scale_y(t + 1)

            scale_y(0)
            run_steps(pool, 0, 2, NT - 2, NT + 1, step3)

        @block.scalar
        def _(act):
            def normalise1(t, j):
                act.wait_ge(ln1_norm, 4 * t + 4)
                wait(act, xt_ps, t - 1)
                nc.scalar.activation(xn[j][:], x_in[j][:], ACT.Identity, bias=ln_nm[j][:], scale=ln_rs[j][:]
                                     ).then_inc(xn_ready, 1)

            def transposed1(t, j):
                wait(act, proj_ps, 3 * (t - 1))
                act.wait_ge(xt_ps, t + 1)
                for h in range(2):
                    last = nc.scalar.copy(xt_h[j][:, 4 * h:4 * h + 4, :].rearrange("p c t -> p (c t)"), bank[h][:])
                last.then_inc(xt_hi, 1)

            def step1(t, j):
                if live(t + 1, 0, NT):
                    transposed1(t + 1, 1 - j)
                if live(t + 2, 0, NT):
                    normalise1(t + 2, j)

            normalise1(0, 0)
            for c in range(KC):
                act.wait_ge(wq_loaded[c % WQ_RING], 16 * (c // WQ_RING + 1))
                nc.scalar.copy(wq_h[:, c, :], wq_raw[c % WQ_RING][:]).then_inc(wq_hi, 1)
                if c == 0:
                    transposed1(0, 0)
                    normalise1(1, 1)
                elif c == 2:
                    transposed1(1, 1)
            normalise1(2, 0)
            normalise1(3, 1)
            transposed1(2, 0)
            run_steps(act, 2, 2, NT - 2, NT, step1)

            def split_att(t):
                act.wait_ge(att_loaded, 16 * t + 16)
                if only(t, 1):
                    nc.scalar.copy(at1_h[:], at_in[:]).then_inc(at_hi, 1)
                else:
                    wait(act, o_ps, 2 * t)
                    nc.scalar.copy(at_h[:], at_in[:]).then_inc(at_hi, 1)

            def stack_to_sbuf(n, j, s):
                act.wait_ge(stack_ps, 5 * n + s + 1)
                dst = k_t[j][0:ST, :] if STACKS[s] == REP else q_t[j][0:ST, STACKS[s], :]
                nc.scalar.copy(dst, bank[0][0:ST, :]).then_inc(stack_sb, 1)

            def shift_to_stack(n, j, h):
                if h % 2 == 0:
                    act.wait_ge(shift_ps, 2 * n + 1 + h // 2)
                nc.scalar.copy(q_t[j][ST:P, h, :], bank[0][HD * h:HD * h + HD, :]).then_inc(shift_sb, 1)

            def piece_hi(n, j):
                act.wait_ge(wo_loaded[j], 16 * (n // 2) + 16)
                nc.scalar.copy(wo_h[:, bass.ds(n * PIECE, PIECE)], wo_raw[j][:]).then_inc(wo_hi, 1)

            def exps(n, j, h, parts):
                for part in parts:
                    i = 3 * h + part
                    if i == 0:
                        wait(act, pv_ps, n - 1)
                    if only(n, 1) and part == 0 and h >= 2:
                        act.wait_ge(qkv_stored[h - 2], 16 * (NT // 2))
                    lo, w = ((0, 512), (512, 384), (896, 512))[part]
                    act.wait_ge(score_ps, UNITS * n + i + 1)
                    nc.scalar.activation(prob[j][:, h, lo:lo + w], bank[4 + i % 2][:, 0:w], ACT.Exp,
                                         scale=INV_SQRT_HD).then_inc(prob_ready, 1)

            def step2(n, j):
                here, after = live(n, 0, NG), live(n + 1, 0, NG)

                def stack_of(s):
                    if after:
                        stack_to_sbuf(n + 1, 1 - j, s)

                def first_stack(s):
                    if live(n + 2, 0, NG):
                        stack_to_sbuf(n + 2, j, s)

                def shift_of(h):
                    if here:
                        shift_to_stack(n, j, h)

                def next_shift_of(h):
                    if after:
                        shift_to_stack(n + 1, 1 - j, h)

                def exps_of(h, *parts):
                    if here:
                        exps(n, j, h, parts)

                exps_of(0, 0, 1)
                shift_of(2)
                shift_of(3)
                exps_of(0, 2)
                stack_of(2)
                exps_of(1, 0, 1)
                if here:
                    piece_hi(n, j)
                stack_of(3)
                exps_of(1, 2)
                if only(n, NG - 1):
                    split_att(0)
                stack_of(4)
                exps_of(2, 0, 1)
                next_shift_of(0)
                exps_of(2, 2)
                next_shift_of(1)
                exps_of(3, 0)
                first_stack(0)
                exps_of(3, 1, 2)
                first_stack(1)

            run_steps(act, -2, 2, NG - 2, NG, step2)
            act.wait_ge(pv_ps, NG - 1)
            split_att(1)

            def normalise_y(t):
                act.wait_ge(y_scale, 8 * t + 4)
                nc.scalar.activation(y[:], y[:], ACT.Identity, bias=ln_nm[0][:], scale=ln_rs[0][:]
                                     ).then_inc(y_norm, 1)

            def normalise_x1(t, j):
                act.wait_ge(y_scale, 8 * t + 8)
                nc.scalar.activation(y[:], x1[j][:], ACT.Identity, bias=ln_nm[0][:], scale=ln_rs[0][:]
                                     ).then_inc(y_norm, 1)

            def transposed2(t):
                act.wait_ge(xt2_ps, t + 1)
                for h in range(2):
                    nc.scalar.copy(xt2_h[:, 4 * h:4 * h + 4, :].rearrange("p c t -> p (c t)"), bank[2 + h][:]
                                   ).then_inc(xt2_hi, 1)

            def gate(t):
                act.wait_ge(gate_step, 12 * t + 2)
                nc.scalar.activation(gate_e[:], logit[:], ACT.Exp, bias=neg_top[:]).then_inc(gate_exp, 1)

            def low_to_sbuf(t):
                act.wait_ge(low_ps, t + 1)
                nc.scalar.copy(low_h[:], bank[7][:, 0:P]).then_inc(low_hi, 1)

            def normalise_z(t, j):
                act.wait_ge(z_scale, 4 * t + 4)
                for cols in final_cols(t):
                    nc.scalar.activation(z[j][:, cols], z[j][:, cols], ACT.Identity, bias=ln_nm[1][:],
                                         scale=ln_rs[1][:]).then_inc(z_norm, 1)

            def step3(t, j):
                if only(t, NT - 1):
                    low_to_sbuf(t - 1)
                if live(t, 1, NT):
                    transposed2(t)
                if live(t - 1, 0, NT):
                    if not only(t, NT - 1):
                        low_to_sbuf(t - 1)
                    normalise_z(t - 1, 1 - j)
                if live(t + 2, 0, NT):
                    split_att(t + 2)
                if live(t + 1, 0, NT):
                    normalise_y(t + 1)
                    normalise_x1(t + 1, 1 - j)
                if live(t, 0, NT):
                    gate(t)

            act.wait_ge(wo_ready, NG)

            def split_ffn(c):
                act.wait_ge(wf_loaded[c % WF_RING], 16 * (c // WF_RING + 1))
                nc.scalar.copy(wf_h[c][:], raw_f[c % WF_RING][:]).then_inc(wf_hi, 1)

            for c in range(EARLY):
                split_ffn(c)
            normalise_y(0)
            act.wait_ge(pv_ps, NG)
            split_ffn(EARLY)
            normalise_x1(0, 0)
            for c in range(EARLY + 1, KC - 1):
                split_ffn(c)
            act.wait_ge(wf_ready, KC - 2)
            transposed2(0)
            split_ffn(KC - 1)
            run_steps(act, 0, 2, NT - 2, NT + 1, step3)

        @block.vector
        def _(dve):
            def statistics(src, j, count, before_it):
                for h in range(2):
                    nc.vector.bn_stats(ln_st[j][:, h, :], src[:, HALF * h:HALF * h + HALF]).then_inc(count, 1)
                wait_apart(dve, count, before_it + 2, FIRST_X)
                nc.vector.bn_aggr(ln_mv[j][:], ln_st[j][:]).then_inc(count, 1)

            def stats1(t, j):
                dve.wait_ge(x_loaded[j], 16 * (t // 2) + 16)
                wait(dve, xn_ready, t - 1)
                statistics(x_in[j], j, ln1_step, 3 * t)

            def lo1(t, j):
                dve.wait_ge(xt_hi, t + 1)
                for h in range(2):
                    part = slice(4 * h, 4 * h + 4)
                    last = nc.vector.tensor_tensor(
                        xt_l[j][:, part, :].rearrange("p c t -> p (c t)"), bank[h][:],
                        xt_h[j][:, part, :].rearrange("p c t -> p (c t)").bitcast(F32), ALU.subtract)
                last.then_inc(xt_ready, 1)

            def bias(t, j, banks=range(3)):
                if 0 in banks:
                    wait(dve, qkv_stored[j], 16 * (t // 2))
                flat = qkv[j][:].rearrange("p g c -> p (g c)")
                for n in banks:
                    dve.wait_ge(proj_ps, 3 * t + n + 1)
                    cols = slice(HALF * n, HALF * n + HALF)
                    nc.vector.tensor_tensor(flat[:, cols], bank[2 + 3 * j + n][:], bq_row[:, cols], ALU.add
                                            ).then_inc(qkv_step, 1)

            def rope(t, j, parts=range(4)):
                qk = qkv[j][:, :, 0:QKW].rearrange("p g (h c) -> p g h c", c=HD)
                half = HD // 2
                tt = t % TT

                def table(tab, lo, hi):
                    row = tab[:, bass.ds(tt, 1), lo:hi]
                    return row.unsqueeze(1).broadcast_to([P, KV, REP + 1, hi - lo])

                for part in parts:
                    if part == 0:
                        dve.wait_ge(qkv_step, 7 * t + 3)
                        last = nc.vector.tensor_tensor(rope_c[:], qk, table(cos_sb, 0, HD), ALU.mult)
                    elif part == 1:
                        last = nc.vector.tensor_tensor(rope_s[:, :, :, 0:half], qk[:, :, :, half:HD],
                                                       table(sin_sb, 0, half), ALU.mult)
                    elif part == 2:
                        last = nc.vector.tensor_tensor(rope_s[:, :, :, half:HD], qk[:, :, :, 0:half],
                                                       table(sin_sb, half, HD), ALU.mult)
                    else:
                        dve.wait_ge(qkv_step, 7 * t + 6)
                        last = nc.vector.tensor_tensor(qk, rope_c[:], rope_s[:], ALU.add)
                    last.then_inc(qkv_step, 1)

            def step1(t, j):
                if live(t + 1, 4, NT):
                    lo1(t + 1, 1 - j)
                if live(t + 2, 5, NT):
                    stats1(t + 2, j)
                bias(t, j)
                rope(t, j)

            stats1(0, 0)
            stats1(1, 1)
            for c in range(KC):
                dve.wait_ge(wq_hi, c + 1)
                nc.vector.tensor_tensor(wq_l[:, c, :], wq_raw[c % WQ_RING][:], wq_h[:, c, :].bitcast(F32),
                                        ALU.subtract).then_inc(wq_ready, 1)
                if c == 0:
                    lo1(0, 0)
                elif c == 2:
                    lo1(1, 1)
                elif c == 6:
                    stats1(2, 0)
            stats1(3, 1)
            lo1(2, 0)
            dve.wait_ge(row_loaded, 16 * N_ROWS)
            bias(0, 0)
            lo1(3, 1)
            stats1(4, 0)
            rope(0, 0)
            bias(1, 1)
            rope(1, 1)
            dve.wait_ge(ident_loaded, 16)
            nc.vector.tensor_copy(ident_r[:], ident[:]).then_inc(const_ready, 1)
            nc.vector.tensor_copy(ident_b[:], ident[:]).then_inc(const_ready, 1)
            nc.vector.tensor_copy(causal_b[:], causal[:]).then_inc(const_ready, 1)
            nc.vector.memset(ones[:], 1.0).then_inc(const_ready, 1)
            for j in range(2):
                nc.vector.memset(k_t[j][ST:P, :].bitcast(F32), 1.0).then_inc(const_ready, 1)
            run_steps(dve, 2, 4, NT - 2, NT - 2, step1)

            def split(n, j):
                dve.wait_ge(grp_loaded[j], 16 * (n // 2) + 16)
                wait(dve, stack_ps, 5 * (n - 1))
                qk = grp[j][:, :, 0:QKW].rearrange("p t (h c) -> p t h c", c=HD)
                q, k = qk[:, :, 0:REP, :], qk[:, :, REP, :]

                def slot(i):
                    return stack[j][:, :, :, HD * i:HD * i + HD]

                nc.vector.tensor_copy(slot(0), qk).then_inc(split_hi, 1)
                nc.vector.tensor_copy(slot(2)[:, :, 0:REP, :], q).then_inc(split_hi, 1)
                nc.vector.tensor_copy(slot(1)[:, :, REP, :], k).then_inc(split_hi, 1)

            def maxima(n, i):
                h, part = i // 3, i % 3
                if part == 0 and h % 2 == 0:
                    wait(dve, shift_step, 4 * n - 2 + h)
                dve.wait_ge(row_ps, UNITS * n + i + 1)
                for qb, at in (((0, 0), (1, 2 * P)), ((2, 0),), ((3, 0),))[part]:
                    last = nc.vector.tensor_reduce(neg_max[:, qb, h:h + 1], bank[1 + part][:, at:at + P * (qb + 1)],
                                                   AX_X, ALU.max, negate=True)
                last.then_inc(row_max_0 if only(n, 0) else row_max, 1)

            def split_maxima(n, half):
                wait(dve, shift_ps, 2 * n + half)
                units = UNITS // 2 * (half + 1)
                if only(n, 0):
                    dve.wait_ge(row_max_0, units)
                else:
                    dve.wait_ge(row_max, UNITS * (n - 1) + units)
                heads = slice(2 * half, 2 * half + 2)
                hi, lo = shift[:, :, heads, 0], shift[:, :, heads, 1]
                nc.vector.tensor_copy(hi, neg_max[:, :, heads]).then_inc(shift_step, 1)
                dve.wait_ge(shift_step, 4 * n + 2 * half + 1)
                nc.vector.tensor_tensor(lo, neg_max[:, :, heads], hi.bitcast(F32), ALU.subtract
                                        ).then_inc(shift_step, 1)

            def turn_denominators(n):
                dve.wait_ge(den_ps, n + 1)
                nc.vector.transpose(den_t[:], bank[7][:]).then_inc(den_step, 1)

            def invert_denominators(n):
                dve.wait_ge(den_step, 3 * n + 1)
                nc.vector.reciprocal(den_r[:], den_t[:, 0:SEQ:HD]).then_inc(den_step, 1)

            def spread_inverses(n):
                dve.wait_ge(den_step, 3 * n + 2)
                nc.vector.transpose(den_i[:].rearrange("p (b c) -> p b c", c=HD),
                                    den_r[:].unsqueeze(2).broadcast_to([P, SEQ // HD, HD])).then_inc(den_step, 1)

            def quotient(n, j):
                dve.wait_ge(den_step, 3 * n + 3)
                dve.wait_ge(pv_ps, n + 1)
                wait(dve, att_stored[j], 16 * (n // 2))
                nc.vector.tensor_tensor(att[j][:], bank[6][:], den_i[:], ALU.mult).then_inc(att_ready, 1)

            def step2(n, j):
                after, before_it = live(n + 1, 0, NG), live(n - 1, 0, NG)

                def maxima_of(*units):
                    if after:
                        for i in units:
                            maxima(n + 1, i)

                if live(n - 2, 0, NG):
                    quotient(n - 2, j)
                maxima_of(0, 1)
                if only(n, 0):
                    bias(NT - 1, 1, (1, 2))
                if live(n + 2, 2, NG):
                    split(n + 2, j)
                maxima_of(2, 3, 4, 5)
                if after:
                    split_maxima(n + 1, 0)
                if only(n, 0):
                    rope(NT - 1, 1, (0,))
                if before_it:
                    turn_denominators(n - 1)
                maxima_of(6)
                if before_it:
                    invert_denominators(n - 1)
                if only(n, 0):
                    rope(NT - 1, 1, (1,))
                maxima_of(7)
                if before_it:
                    spread_inverses(n - 1)
                maxima_of(8)
                if only(n, 0):
                    rope(NT - 1, 1, (2,))
                maxima_of(9, 10, 11)
                if after:
                    split_maxima(n + 1, 1)
                if only(n, 0):
                    rope(NT - 1, 1, (3,))

            split(0, 0)
            lo1(NT - 1, 1)
            bias(NT - 2, 0)
            nc.vector.memset(shift[:].bitcast(F32), 0.0).then_inc(const_ready, 1)
            dve.wait_ge(const_ready, 7)
            rope(NT - 2, 0)
            split(1, 1)
            bias(NT - 1, 1, (0,))
            step2(-1, 1)
            step2(0, 0)
            run_steps(dve, 1, 4, NG - 2, NG, step2)

            def split_att(t):
                dve.wait_ge(at_hi, t + 1)
                hi, lo = (at1_h, at1_l) if only(t, 1) else (at_h, at_l)
                nc.vector.tensor_tensor(lo[:], at_in[:], hi[:].bitcast(F32), ALU.subtract).then_inc(at_ready, 1)

            split_att(0)
            quotient(NG - 2, 0)
            split_att(1)

            def project_bias(t, n):
                if n == 0:
                    wait(dve, xt2_ps, t)
                dve.wait_ge(o_ps, 2 * t + n + 1)
                cols = slice(HALF * n, HALF * n + HALF)
                nc.vector.tensor_tensor(y[:, cols], bank[n][:], bo_row[:, cols], ALU.add).then_inc(y_step, 1)

            def project_sum(t):
                for n in range(1 if only(t, 1) else 0, 2):
                    project_bias(t, n)
                dve.wait_ge(y_step, 9 * t + 2)
                statistics(y, 0, y_step, 9 * t + 2)

            def residual1(t, j):
                s = 9 * t
                dve.wait_ge(res_loaded, 16 * t + 16)
                dve.wait_ge(y_norm, 2 * t + 1)
                wait(dve, z_step, 7 * (t - 1))
                nc.vector.tensor_tensor(x1[j][:], y[:], x_res[:], ALU.add).then_inc(y_step, 1)
                dve.wait_ge(y_step, s + 6)
                statistics(x1[j], 0, y_step, s + 6)

            def lo2(t):
                for h in range(2):
                    dve.wait_ge(xt2_hi, 2 * t + h + 1)
                    part = slice(4 * h, 4 * h + 4)
                    nc.vector.tensor_tensor(
                        xt2_l[:, part, :].rearrange("p c t -> p (c t)"), bank[2 + h][:],
                        xt2_h[:, part, :].rearrange("p c t -> p (c t)").bitcast(F32), ALU.subtract
                        ).then_inc(xt2_ready, 1)

            def gate(t):
                s = 12 * t

                def step(ins):
                    ins.then_inc(gate_step, 1)

                dve.wait_ge(ffn_ps, 3 * t + 1)
                step(nc.vector.tensor_copy(logit[:], bank[4][:, 0:EXP]))
                dve.wait_ge(gate_step, s + 1)
                mine = logit[:].unsqueeze(2).broadcast_to([P, EXP, EXP])
                other = logit[:].unsqueeze(1).broadcast_to([P, EXP, EXP])
                step(nc.vector.tensor_reduce(neg_top[:], logit[:], AX_X, ALU.max, negate=True))
                step(nc.vector.tensor_tensor(equal[:], other, mine, ALU.is_equal))
                step(nc.vector.tensor_tensor(later[:], other, mine, ALU.is_gt))
                dve.wait_ge(gate_step, s + 4)
                step(nc.vector.tensor_tensor(equal[:], equal[:], before[:], ALU.mult))
                dve.wait_ge(gate_step, s + 5)
                step(nc.vector.tensor_tensor(later[:], later[:], equal[:], ALU.add))
                dve.wait_ge(gate_step, s + 6)
                step(nc.vector.tensor_reduce(rank[:], later[:], AX_X, ALU.add))
                dve.wait_ge(gate_step, s + 7)
                dve.wait_ge(gate_exp, t + 1)
                step(nc.vector.scalar_tensor_tensor(out=gate_w[:], in0=rank[:], scalar=1.5, in1=gate_e[:],
                                                    op0=ALU.is_lt, op1=ALU.mult))
                dve.wait_ge(gate_step, s + 8)
                step(nc.vector.tensor_reduce(gate_s[:], gate_w[:], AX_X, ALU.add))
                dve.wait_ge(gate_step, s + 9)
                step(nc.vector.reciprocal(gate_r[:], gate_s[:]))
                dve.wait_ge(gate_step, s + 10)
                step(nc.vector.tensor_scalar(gate_w[:], gate_w[:], gate_r[:], SCALING, ALU.mult, ALU.mult))
                dve.wait_ge(gate_step, s + 11)
                wait(dve, low_ps, t)
                step(nc.vector.tensor_tensor(low[:], bank[4][:, EXP:AGW].rearrange("p (e r) -> p e r", r=RANK),
                                             gate_w[:].unsqueeze(2).broadcast_to([P, EXP, RANK]), ALU.mult))

            def low_lo(t):
                dve.wait_ge(low_hi, t + 1)
                nc.vector.tensor_tensor(low_l[:], bank[7][:, 0:P], low_h[:].bitcast(F32), ALU.subtract
                                        ).then_inc(low_ready, 1)

            def ffn_sum(t, j):
                s = 7 * t
                dve.wait_ge(lora_ps, t + 1)
                wait(dve, out_stored[j], 16 * (t // 2))
                for b, (at, w) in enumerate(FFN_COLS):
                    lo = max(at, AGW)
                    cols = slice(lo - AGW, at + w - AGW)
                    nc.vector.tensor_tensor(z[j][:, cols], bank[4 + b][:, lo - at:w], bf_row[:, cols], ALU.add
                                            ).then_inc(z_step, 1)
                dve.wait_ge(z_step, s + 3)
                statistics(z[j], 1, z_step, s + 3)

            def residual2(t, j):
                for i, cols in enumerate(final_cols(t)):
                    dve.wait_ge(z_norm, t + 1 + i)
                    nc.vector.tensor_tensor(z[j][:, cols], z[j][:, cols], x1[j][:, cols], ALU.add).then_inc(z_step, 1)

            def step3(t, j):
                if only(t, NT - 1):
                    low_lo(t - 1)
                if live(t, 1, NT):
                    lo2(t)
                if live(t - 1, 0, NT):
                    if not only(t, NT - 1):
                        low_lo(t - 1)
                    ffn_sum(t - 1, 1 - j)
                if live(t + 1, 0, NT):
                    project_sum(t + 1)
                if live(t - 1, 0, NT):
                    residual2(t - 1, 1 - j)
                if live(t + 2, 0, NT):
                    split_att(t + 2)
                if live(t + 1, 0, NT):
                    residual1(t + 1, 1 - j)
                if live(t, 0, NT):
                    gate(t)

            dve.wait_ge(late_loaded, 16 * N_LATE)

            def split_ffn(c):
                dve.wait_ge(wf_hi, c + 1)
                nc.vector.tensor_tensor(wf_l[c][:], raw_f[c % WF_RING][:], wf_h[c][:].bitcast(F32), ALU.subtract
                                        ).then_inc(wf_ready, 1)

            for c in range(EARLY):
                split_ffn(c)
            project_sum(0)
            residual1(0, 0)
            turn_denominators(NG - 1)
            invert_denominators(NG - 1)
            spread_inverses(NG - 1)
            quotient(NG - 1, 1)
            for c in range(EARLY, KC - 2):
                split_ffn(c)
            project_bias(1, 0)
            lo2(0)
            for c in range(KC - 2, KC):
                split_ffn(c)
            for j in range(2):
                dve.wait_ge(att_stored[j], 16 * (NG // 2))
            run_steps(dve, 0, 4, NT - 2, NT + 1, step3)

        @block.tensor
        def _(pe):
            mm = nc.tensor.matmul

            def product(dst, a_h, a_l, w_h, w_l, start, stop):
                mm(dst, a_h, w_h, start=start, stop=False, skip_group_check=True)
                mm(dst, a_l, w_h, start=False, stop=False, skip_group_check=True)
                return mm(dst, a_h, w_l, start=False, stop=stop, skip_group_check=True)

            def transpose1(t, j):
                pe.wait_ge(xn_ready, t + 1)
                wait(pe, xt_ready, t)
                for c in range(KC):
                    last = nc.tensor.transpose(bank[c // 4][:, P * (c % 4):P * (c % 4) + P],
                                               xn[j][:, P * c:P * c + P], ident[:])
                last.then_inc(xt_ps, 1)

            def project_chunk(t, j, n, c):
                cols = slice(HALF * n, HALF * n + HALF)
                return product(bank[2 + 3 * j + n][:], xt_h[j][:, c, :], xt_l[j][:, c, :],
                               wq_h[:, c, cols], wq_l[:, c, cols], c == 0, c == KC - 1)

            def project_part(t, j, c):
                if c == 0:
                    pe.wait_ge(xt_ready, t + 1)
                pe.wait_ge(wq_ready, c + 1)
                for n in range(3):
                    last = project_chunk(t, j, n, c)
                    if c == KC - 1:
                        last.then_inc(proj_ps, 1)

            def project_bank(t, j, n):
                if n == 0:
                    pe.wait_ge(xt_ready, t + 1)
                pe.wait_ge(qkv_step, 7 * (t - 2) + n + 1)
                for c in range(KC):
                    last = project_chunk(t, j, n, c)
                last.then_inc(proj_ps, 1)

            def step1(t, j):
                transpose1(t + 1, 1 - j)
                for n in range(3):
                    project_bank(t, j, n)

            pe.wait_ge(ident_loaded, 16)
            transpose1(0, 0)
            project_part(0, 0, 0)
            transpose1(1, 1)
            project_part(0, 0, 1)
            for c in range(2, KC):
                project_part(0, 0, c)
                project_part(1, 1, c - 2)
            transpose1(2, 0)
            for c in range(KC - 2, KC):
                project_part(1, 1, c)
            run_steps(pe, 2, 2, NT - 2, NT - 1, step1)

            def stack_transpose(n, j, s):
                if s == 0:
                    pe.wait_ge(split_hi, 3 * n + 3)
                    pe.wait_ge(split_lo, 2 * n + 2)
                if s == 0:
                    wait(pe, shift_sb, 4 * n - 2)
                elif s == 2:
                    wait(pe, shift_sb, 4 * n)
                else:
                    pe.wait_ge(stack_sb, 5 * n + s)
                head = STACKS[s]
                for tt in range(TT):
                    last = nc.tensor.transpose(bank[0][0:ST, P * tt:P * tt + P].bitcast(F32R),
                                               stack[j][:, tt, head, :], ident_r[:])
                last.then_inc(stack_ps, 1)

            def shift_transpose(n, half):
                pe.wait_ge(shift_step, 4 * n + 2 * half + 2)
                if half == 0:
                    pe.wait_ge(stack_sb, 5 * n + 5)
                else:
                    pe.wait_ge(stack_sb, 5 * n + (5 if only(n, NG - 1) else 7))
                for tt in range(TT):
                    last = nc.tensor.transpose(bank[0][:, P * tt:P * tt + P].bitcast(F32R),
                                               shift[:, tt, :, :].rearrange("p h c -> p (h c)"), ident_r[:])
                last.then_inc(shift_ps, 1)

            def row_scores(before_it, j, pair):
                h, units = pair // 2, ((0,), (1, 2))[pair % 2]
                if units[0] == 0:
                    pe.wait_ge(stack_sb, 5 * before_it + 7 + h)
                masked = []
                for part in units:
                    count = 3 * h + part - 2
                    if not isinstance(before_it, int) or UNITS * before_it + count > 0:
                        pe.wait_ge(row_max, UNITS * before_it + count)
                    else:
                        wait(pe, row_max_0, UNITS * (before_it + 1) + count)
                    for qb, at in (((0, 0), (1, 2 * P)), ((2, 0),), ((3, 0),))[part]:
                        w = max(P * (qb + 1), 2 * P)
                        mm(bank[1 + part][:, at:at + w], q_t[j][0:ST, h, P * qb:P * qb + P], k_t[j][0:ST, 0:w],
                           start=True, stop=False, skip_group_check=True)
                        masked.append((part, at + P * qb))
                for i, (part, at) in enumerate(masked):
                    last = mm(bank[1 + part][:, at:at + P], ident_b[:], causal_b[:], start=False, stop=True,
                              skip_group_check=True)
                    if part or i == 1:
                        last.then_inc(row_ps, 1)

            def scores(n, j, i):
                h, part = i // 3, i % 3
                if part == 0:
                    pe.wait_ge(shift_sb, 4 * n + h + 1)
                if only(n, 0) and i == 1:
                    pe.wait_ge(qkv_step, 7 * (NT - 1) + 1)
                wait(pe, prob_ready, UNITS * n + i - 1)
                for kc, at, q0 in (((0, 0, 0),), ((1, 0, P),), ((2, 0, 2 * P), (3, 2 * P, 2 * P)))[part]:
                    w = SEQ - q0
                    last = mm(bank[4 + i % 2][:, at:at + w], k_t[j][:, P * kc:P * kc + P], q_t[j][:, h, q0:SEQ],
                              start=True, stop=True, skip_group_check=True)
                last.then_inc(score_ps, 1)

            def weigh(n, j, kc):
                if kc == 0:
                    wait(pe, att_ready, n)
                    pe.wait_ge(v_loaded[j], 16 * (n // 2) + 16)
                at = (0, 512, 896, 1280)[kc]
                for h in range(REP):
                    last = mm(bank[6][HD * h:HD * h + HD, P * kc:SEQ], v_sb[j][:, kc, :],
                              prob[j][:, h, at:at + SEQ - P * kc], start=(kc == 0), stop=(kc == TT - 1),
                              skip_group_check=True)
                if kc == TT - 1:
                    last.then_inc(pv_ps, 1)

            def denominators(n, j, i):
                if i == 0:
                    if only(n, 0):
                        pe.wait_ge(qkv_step, 7 * (NT - 1) + 3)
                    pe.wait_ge(prob_masked, 8 * n + 8)
                    wait(pe, den_step, 3 * n - 2)
                elif i == 2:
                    pe.wait_ge(prob_summed, 8 * n + 8)
                cols = (slice(0, SEQ), slice(P, 2 * P), slice(2 * P, SEQ))[i]
                for h in range(REP):
                    what = (prob[j][:, h, 0:512], prob[j][:, h, 512:640], key_sum[j][:, h, :])[i]
                    last = mm(bank[7][HD * h:HD * h + HD, cols], ones[:], what, start=(i == 0), stop=(i == 2),
                              skip_group_check=True)
                if i == 2:
                    last.then_inc(den_ps, 1)

            order = ("C0 C1 R0 D0 U0 C2 R1 D1 D2 S2 C3 C4 V0 R2 S3 C5 R3 S4 C6 C7 R4 V1 "
                     "T0 C8 R5 C9 V2 N0 C10 R6 C11 N1 R7 V3").split()

            def unit(what, n, j):
                kind, i = what[0], int(what[1:])
                if kind == "S" and live(n + 1, 0, NG):
                    stack_transpose(n + 1, 1 - j, i)
                if kind == "N" and live(n + 2, 0, NG):
                    stack_transpose(n + 2, j, i)
                if kind == "R" and live(n + 1, 0, NG):
                    row_scores(n, 1 - j, i)
                if kind == "T" and live(n + 1, 0, NG):
                    shift_transpose(n + 1, 0)
                if kind == "U" and live(n, 0, NG):
                    shift_transpose(n, 1)
                if kind == "C" and live(n, 0, NG):
                    scores(n, j, i)
                if kind == "D" and live(n - 1, 0, NG):
                    denominators(n - 1, 1 - j, i)
                if kind == "V" and live(n - 1, 0, NG):
                    weigh(n - 1, 1 - j, i)

            def step2(n, j):
                for what in order:
                    unit(what, n, j)

            pe.wait_ge(const_ready, 6)
            pe.wait_ge(xt_ready, NT)
            unit("N0", -2, 0)
            project_bank(NT - 1, 1, 0)
            unit("N1", -2, 0)
            pe.wait_ge(qkv_step, 7 * (NT - 2) + 3)
            last_tile = [(n, c) for n in range(1, 3) for c in range(KC)]
            for what in order:
                if what[0] in "RSTN":
                    unit(what, -1, 1)
                for n, c in last_tile[:2 if what[0] == "R" else what in ("S2", "S3", "S4")]:
                    last = project_chunk(NT - 1, 1, n, c)
                    if c == KC - 1:
                        last.then_inc(proj_ps, 1)
                    last_tile.remove((n, c))
            for n, c in last_tile:
                last = project_chunk(NT - 1, 1, n, c)
            if last_tile:
                last.then_inc(proj_ps, 1)
            run_steps(pe, 0, 2, NG - 2, NG, step2)

            def project_out(t, n):
                if n == 0:
                    pe.wait_ge(at_ready, t + 1)
                wait(pe, y_step, 9 * (t - 1) + n + 1)
                for c in range(KC):
                    cols = slice(D * c + HALF * n, D * c + HALF * n + HALF)
                    hi, lo = (at1_h, at1_l) if only(t, 1) else (at_h, at_l)
                    last = product(bank[n][:], hi[:, c, :], lo[:, c, :], wo_h[:, cols], wo_l[:, cols],
                                   c == 0, c == KC - 1)
                last.then_inc(o_ps, 1)

            def transpose2(t):
                pe.wait_ge(y_norm, 2 * t + 2)
                wait(pe, xt2_ready, 2 * t)
                for c in range(KC):
                    last = nc.tensor.transpose(bank[2 + c // 4][:, P * (c % 4):P * (c % 4) + P],
                                               y[:, P * c:P * c + P], ident[:])
                last.then_inc(xt2_ps, 1)

            def ffn(t):
                wait(pe, z_step, 7 * (t - 1) + 3)
                for b, (at, w) in enumerate(FFN_COLS):
                    for c in range(KC):
                        if b == 0 and c % 4 == 0:
                            pe.wait_ge(xt2_ready, 2 * t + c // 4 + 1)
                        if isinstance(t, int) and t == 0 and b == 0:
                            pe.wait_ge(wf_ready, c + 1)
                        last = product(bank[4 + b][:, 0:w], xt2_h[:, c, :], xt2_l[:, c, :], wf_h[c][:, at:at + w],
                                       wf_l[c][:, at:at + w], c == 0, False)
                    last.then_inc(ffn_ps, 1)

            def transpose_low(t):
                pe.wait_ge(gate_step, 12 * t + 12)
                wait(pe, low_ready, t)
                nc.tensor.transpose(bank[7][:, 0:P], low[:].rearrange("p e r -> p (e r)"), ident[:]).then_inc(low_ps, 1)

            def lora(t):
                pe.wait_ge(low_ready, t + 1)
                for b, (at, w) in enumerate(FFN_COLS):
                    lo = max(at, AGW)
                    cols = slice(KC * D + lo - AGW, KC * D + at + w - AGW)
                    last = product(bank[4 + b][:, lo - at:w], low_h[:], low_l[:], wo_h[:, cols], wo_l[:, cols],
                                   False, True)
                last.then_inc(lora_ps, 1)

            def step3(t, j):
                if only(t, NT - 1):
                    transpose_low(t - 1)
                if live(t, 1, NT):
                    transpose2(t)
                if not only(t, NT - 1) and live(t - 1, 0, NT):
                    transpose_low(t - 1)
                if live(t + 1, 2, NT):
                    project_out(t + 1, 0)
                if live(t - 1, 0, NT):
                    lora(t - 1)
                if live(t + 1, 2, NT):
                    project_out(t + 1, 1)
                ffn(t)

            pe.wait_ge(wo_ready, NG)
            pe.wait_ge(shift_sb, 4 * NG)
            for n in range(2):
                project_out(0, n)
            step2(NG, 0)
            project_out(1, 0)
            transpose2(0)
            project_out(1, 1)
            pe.wait_ge(att_ready, NG)
            run_steps(pe, 0, 2, NT - 2, NT, step3)
            transpose_low(NT - 1)
            lora(NT - 1)


def kernel(L0_attn_x, L0_attn_w_qkv, L0_attn_b_qkv, L0_attn_w_o, L0_attn_b_o, L0_ffn_gate_w, L0_ffn_base_w,
           L0_ffn_base_b, L0_ffn_lora_A, L0_ffn_lora_B):
    import numpy as np
    import concourse.bacc as bacc
    from concourse import mybir as mb
    from concourse.bass_utils import run_bass_kernel_spmd

    halves = np.concatenate([np.arange(0, HD, 2), np.arange(1, HD, 2)])
    order = []
    for g in range(KV):
        for h in range(REP):
            order.append((REP * g + h) * HD + halves)
        order.append(HEADS * HD + g * HD + halves)
        order.append((HEADS + KV) * HD + g * HD + np.arange(HD))
    order = np.concatenate(order)

    def by_partition(w_t):
        return np.ascontiguousarray(w_t.reshape(KC, P, -1).transpose(1, 0, 2))

    arr = {k: np.asarray(v) for k, v in locals().items() if k.startswith("L0_")}
    w_qkv = by_partition(arr["L0_attn_w_qkv"][order].T)
    w_o = by_partition(arr["L0_attn_w_o"].T).reshape(P, KC * D)
    lora_b = arr["L0_ffn_lora_B"].transpose(0, 2, 1).reshape(ER, D)
    w_ffn = np.concatenate([arr["L0_ffn_gate_w"].T, arr["L0_ffn_lora_A"].reshape(ER, D).T, arr["L0_ffn_base_w"].T], 1)

    inv = np.float32(1.0) / np.float32(10000.0) ** (np.arange(0, HD, 2, dtype=np.float32) / np.float32(HD))
    ang = np.arange(SEQ, dtype=np.float32)[:, None] * inv[None, :].astype(np.float32)
    cos, sin = np.cos(ang).astype(np.float32), np.sin(ang).astype(np.float32)

    def table(t):
        return np.ascontiguousarray(t.reshape(TT, P, HD).transpose(1, 0, 2))

    inputs = {
        "x": np.ascontiguousarray(arr["L0_attn_x"].reshape(NT, P, D)),
        "w_qkv": w_qkv,
        "b_qkv": np.ascontiguousarray(arr["L0_attn_b_qkv"][order][None]),
        "w_out": np.ascontiguousarray(np.concatenate([w_o, lora_b], 1)),
        "b_o": np.ascontiguousarray(arr["L0_attn_b_o"][None]),
        "w_ffn": by_partition(w_ffn),
        "b_ffn": np.ascontiguousarray(arr["L0_ffn_base_b"][None]),
        "cos_t": table(np.concatenate([cos, cos], 1)),
        "sin_t": table(np.concatenate([-sin, sin], 1)),
        "ident": np.eye(P, dtype=np.float32),
        "causal": np.where(np.tril(np.ones((P, P), bool)), 0.0, MASKED).astype(np.float32),
        "before": np.tril(np.ones((EXP, EXP), np.float32), -1)[None],
    }
    nc = bacc.Bacc("TRN2", target_bir_lowering=False, num_devices=1)
    aps = [nc.dram_tensor(k, v.shape, mb.dt.from_np(v.dtype), kind="ExternalInput").ap() for k, v in inputs.items()]
    out = nc.dram_tensor("out", (NT, P, D), mb.dt.float32, kind="ExternalOutput").ap()
    build(nc, *aps, out)
    result = run_bass_kernel_spmd(nc, [inputs], core_ids=[0])
    return result.results[0]["out"].reshape(BATCH, SEQ, D)
```
